# Optimizing a Trainium2 kernel written in Bass

```python
import numpy as np
import jax
import jax.numpy as jnp

def _softmax(x, axis=-1):
    return jax.nn.softmax(x, axis=axis)

def _gelu(x):
    return jax.nn.gelu(x, approximate=True)

def _silu(x):
    return jax.nn.silu(x)

def _sigmoid(x):
    return jax.nn.sigmoid(x)

def _layernorm(x, axis=-1, eps=1e-05):
    m = jnp.mean(x, axis=axis, keepdims=True)
    v = jnp.var(x, axis=axis, keepdims=True)
    return (x - m) / jnp.sqrt(v + eps)

def _scatter_add(tgt, idx, src, axis=0):
    return tgt.at[idx].add(src)

def _segment_sum(src, seg, n):
    return jax.ops.segment_sum(src, seg, n)
kernel_name = 'mk_flamingo_gated_d1_seqx_r4_ee61b5'

def setup_inputs(seed: int=0):
    np.random.seed(seed)
    _w = jnp.asarray

    def _rec_inputs():
        import jax
        import jax.numpy as jnp
        _rk = jax.random.key(seed)
        x = -0.0002928 + 1 * jax.random.normal(jax.random.fold_in(_rk, 1), (4, 512, 256), jnp.float32)
        _lenS = 512 - jax.random.randint(jax.random.fold_in(_rk, 7), (4,), 0, max(1, 512 // 4) + 1, jnp.int32)
        _lenS2 = 512 - jax.random.randint(jax.random.fold_in(_rk, 8), (4,), 0, max(1, 512 // 4) + 1, jnp.int32)
        _ctx_1024P = jax.random.normal(jax.random.fold_in(_rk, 11), (4, 16, 256), jnp.float32)
        _ctx_1024c = jax.random.dirichlet(jax.random.fold_in(_rk, 511), 0.3 * jnp.ones((16,), jnp.float32), (4, 512))
        _ctx_1024t = jnp.einsum('bsk,bkd->bsd', _ctx_1024c, _ctx_1024P)
        _ctx_1024t = _ctx_1024t * jax.lax.rsqrt(jnp.mean(jnp.square(_ctx_1024t)) + 1e-12) * 0.953939
        ctx_1024 = -1.39393e-06 + 0.999914 * (_ctx_1024t + 0.3 * jax.random.normal(jax.random.fold_in(_rk, 611), (4, 512, 256), jnp.float32))
        _g = jax.random.normal(jax.random.fold_in(_rk, 9001), (2, 1), jnp.float32)
        _g = jnp.sign(_g) * jnp.maximum(jnp.abs(_g), 1.0) + (_g == 0) * 1.0
        g_xattn = _g[0]
        g_ffn = _g[1]
        return (x, ctx_1024, g_xattn, g_ffn)
    x, ctx_1024, g_xattn, g_ffn = _rec_inputs()

    def _L0_xattn_setup():
        import jax, jax.numpy as jnp
        import numpy as np
        B, T, N_EMBD, N_HEAD = (2, 512, 256, 16)
        HEAD = N_EMBD // N_HEAD
        WINDOW = 64
        key = jax.random.key(seed)
        kq, kk, kv, kw = jax.random.split(key, 4)
        q = jax.random.normal(kq, (B, T, N_EMBD), dtype=jnp.float32)
        k = jax.random.normal(kk, (B, T, N_EMBD), dtype=jnp.float32)
        v = jax.random.normal(kv, (B, T, N_EMBD), dtype=jnp.float32)
        W_proj = jax.random.normal(kw, (N_EMBD, N_EMBD), dtype=jnp.float32) * (1.0 / np.sqrt(N_EMBD))
        b_proj = jnp.zeros((N_EMBD,), dtype=jnp.float32)
        return {'q': q, 'k': k, 'v': v, 'W_proj': W_proj, 'b_proj': b_proj}
    _L0_xattn_all = _L0_xattn_setup()
    _L0_xattn_in = {k: v for k, v in _L0_xattn_all.items() if k in ('W_proj', 'b_proj')}
    del _L0_xattn_all

    def _L0_ffn_setup():
        import jax, jax.numpy as jnp
        import numpy as np
        B, T, D, I, E, K = (2, 512, 256, 512, 8, 2)
        key = jax.random.key(seed)
        ks = jax.random.split(key, 5)
        s_d = 1.0 / np.sqrt(D)
        s_i = 1.0 / np.sqrt(I)
        return {'x': jax.random.normal(ks[0], (B, T, D), dtype=jnp.float32), 'Wg': jax.random.normal(ks[1], (E, D), dtype=jnp.float32) * s_d, 'W1': jax.random.normal(ks[2], (E, I, D), dtype=jnp.float32) * s_d, 'W2': jax.random.normal(ks[3], (E, I, D), dtype=jnp.float32) * s_d, 'W3': jax.random.normal(ks[4], (E, D, I), dtype=jnp.float32) * s_i}
    _L0_ffn_all = _L0_ffn_setup()
    _L0_ffn_in = {k: v for k, v in _L0_ffn_all.items() if k in ('Wg', 'W1', 'W2', 'W3')}
    del _L0_ffn_all
    return {'x': x, 'ctx_1024': ctx_1024, 'g_xattn': g_xattn, 'g_ffn': g_ffn, 'L0_xattn_W_proj': _L0_xattn_in['W_proj'], 'L0_xattn_b_proj': _L0_xattn_in['b_proj'], 'L0_ffn_Wg': _L0_ffn_in['Wg'], 'L0_ffn_W1': _L0_ffn_in['W1'], 'L0_ffn_W2': _L0_ffn_in['W2'], 'L0_ffn_W3': _L0_ffn_in['W3']}

def reference(x, ctx_1024, g_xattn, g_ffn, L0_xattn_W_proj, L0_xattn_b_proj, L0_ffn_Wg, L0_ffn_W1, L0_ffn_W2, L0_ffn_W3):
    import jax
    import jax.numpy as jnp

    def _L0_xattn_ref(q, k, v, W_proj, b_proj):
        import jax, jax.numpy as jnp
        import numpy as np
        B, T, N_EMBD, N_HEAD = (2, 512, 256, 16)
        HEAD = N_EMBD // N_HEAD
        WINDOW = 64
        Bsz, Tlen, _ = q.shape
        qh = q.reshape(Bsz, Tlen, N_HEAD, HEAD).transpose(0, 2, 1, 3)
        kh = k.reshape(Bsz, Tlen, N_HEAD, HEAD).transpose(0, 2, 1, 3)
        vh = v.reshape(Bsz, Tlen, N_HEAD, HEAD).transpose(0, 2, 1, 3)
        scale = 1.0 / np.sqrt(HEAD)
        scores = jnp.einsum('bhqd,bhkd->bhqk', qh, kh) * scale
        idx = jnp.arange(Tlen)
        dist = jnp.abs(idx[None, :] - idx[:, None])
        scores = jnp.where(dist[None, None] > WINDOW, -jnp.inf, scores)
        attn = jax.nn.softmax(scores, axis=-1)
        y = jnp.einsum('bhqk,bhkd->bhqd', attn, vh)
        y = y.transpose(0, 2, 1, 3).reshape(Bsz, Tlen, N_EMBD)
        return y @ W_proj.T + b_proj

    def _L0_ffn_ref(x, Wg, W1, W2, W3):
        import jax, jax.numpy as jnp
        import numpy as np
        B, T, D, I, E, K = (2, 512, 256, 512, 8, 2)
        scores = jnp.einsum('btd,ed->bte', x, Wg)
        topk_scores, topk_idx = jax.lax.top_k(scores, K)
        topk_probs = jax.nn.softmax(topk_scores, axis=-1)
        h1 = jnp.einsum('btd,eid->btei', x, W1)
        h2 = jnp.einsum('btd,eid->btei', x, W2)
        h = jax.nn.silu(h1) * h2
        expert_out = jnp.einsum('btei,edi->bted', h, W3)
        gating = jnp.sum(jax.nn.one_hot(topk_idx, E, dtype=x.dtype) * topk_probs[..., None], axis=-2)
        return jnp.einsum('bte,bted->btd', gating, expert_out)
    x = x + jnp.tanh(g_xattn[0]) * _L0_xattn_ref(_layernorm(x, axis=-1), ctx_1024, ctx_1024, L0_xattn_W_proj, L0_xattn_b_proj)
    x = x + jnp.tanh(g_ffn[0]) * _L0_ffn_ref(_layernorm(x, axis=-1), L0_ffn_Wg, L0_ffn_W1, L0_ffn_W2, L0_ffn_W3)
    return x

_drawn_inputs = setup_inputs


def setup_inputs(seed=0):
    import zlib

    import numpy as np

    out = dict(_drawn_inputs(seed))
    spreads = {'L0_xattn_b_proj': (0.0, 0.1)}
    factors = {}
    for name, (base, spread) in spreads.items():
        noise = np.random.default_rng([zlib.crc32(name.encode()), seed]).standard_normal(out[name].shape)
        drawn = base * np.exp(spread * noise) if base else spread * noise
        out[name] = jnp.asarray(drawn.astype(out[name].dtype))
    for name, factor in factors.items():
        out[name] = (out[name] * factor).astype(out[name].dtype)
    return out
```

```python
from contextlib import ExitStack

import numpy as np
import concourse.bass as bass
from concourse import mybir

F32 = mybir.dt.float32
BF16 = mybir.dt.bfloat16
U32 = mybir.dt.uint32
I32 = mybir.dt.int32
ALU = mybir.AluOpType
ACT = mybir.ActivationFunctionType
AX = mybir.AxisListType

P = 128
B, T, D = 4, 512, 256
H, HD, WINDOW = 16, 16, 64
E, FI, TOPK = 8, 512, 2
NTOK = B * T
TPB = T // P
NT = NTOK // P
DB, FB = D // P, FI // P
EPS = 1e-5
Q_SCALE = 1.0 / HD ** 0.5
QUAD = 32
BAND = QUAD + 2 * WINDOW
PARTS = 6 * HD
ROWS = PARTS + 3
GROUP = 4
NG = H // GROUP
NEG = -1e30

REGION = NTOK + P
NTILES = NTOK * TOPK // P + E - 1
SPARE = E - 1
ROW = D + 2
SLOTS = TOPK * NTOK

C_ID, C_MS, C_MT = 0, P, P + 3 * BAND
C_UP = C_MT + 2 * P
C_ONE = C_UP + P
NCB = C_ONE + P
C_IOTA, C_REG = NCB, NCB + E
C_TILE = C_REG + E
C_DEST = C_TILE + NTILES
C_P = C_DEST + NT
NCF = C_P + 1

SHEADS = [(0, 3), (3, 3), (6, 3), (9, 3), (12, 2), (14, 2)]
NS = len(SHEADS)
STACK_BUFS, P_BUFS = 3, 3


def constants():
    c = np.zeros((P, NCF), np.float32)
    p = np.arange(P)
    c[:, C_ID:C_ID + P] = np.eye(P)
    for kind in range(3):
        ms = c[:, C_MS + kind * BAND:C_MS + (kind + 1) * BAND]
        col = np.arange(BAND)[None, :]
        q = (p % QUAD)[:, None]
        ms[(col < q) | (col > q + 2 * WINDOW)] = NEG
        key = (p // QUAD * QUAD)[:, None] - WINDOW + col
        if kind == 0:
            ms[key < 0] = NEG
        if kind == 2:
            ms[key >= P] = NEG
    col = np.arange(2 * P)[None, :]
    mt = c[:, C_MT:C_MT + 2 * P]
    mt[(col < p[:, None]) | (col > p[:, None] + 2 * WINDOW)] = NEG
    c[:, C_UP:C_UP + P] = p[:, None] < p[None, :]
    c[:, C_ONE:C_ONE + P] = 1.0
    c[:, C_IOTA:C_IOTA + E] = np.arange(E)
    c[:, C_REG:C_REG + E] = np.arange(E) * REGION
    c[:, C_TILE:C_TILE + NTILES] = np.arange(NTILES)
    c[:, C_DEST:C_DEST + NT] = TOPK * (np.arange(NT)[None, :] * P + p[:, None])
    c[:, C_P] = p
    pad = np.zeros((E + SPARE, P, ROW), np.float32)
    pad[:, :, D] = SLOTS + np.arange(E + SPARE)[:, None] * P + p[None, :]
    return c, pad


def schedule():
    steps = [("ln1", 0), ("ln1", 1)]
    for n in range(2 * TPB):
        steps.append(("prep", n))
    for t in range(TPB):
        steps.append(("smax", 0, t, 0))
        steps.append(("smax", 0, t, 1))
    steps += [("mrow", 0)]
    for b in range(B):
        if b + 2 < B:
            steps.append(("ln1", b + 2))
        for v in range(4 * NG):
            steps.append(("score", b, v))
            if v >= 1:
                steps.append(("pv", b, v - 1))
                if v % 4 == 0:
                    steps.append(("yout", b, v // 4 - 1))
                if v % 4 == 1 and v > 1:
                    steps.append(("yturn", b, v // 4 - 1))
                    steps.append(("ynorm", b, v // 4 - 1))
            elif b > 0:
                steps.append(("pv", b - 1, 4 * NG - 1))
                steps.append(("yout", b - 1, NG - 1))
            if b > 0:
                steps += post(b - 1, v)
            if b + 1 < B:
                if v < 8:
                    steps.append(("prep", 8 * (b + 1) + v))
                elif v < 12:
                    steps.append(("smax", b + 1, v - 8, 0))
                    steps.append(("smax", b + 1, v - 8, 1))
                elif v == 12:
                    steps.append(("mrow", b + 1))
    steps.append(("pv", B - 1, 4 * NG - 1))
    steps.append(("yout", B - 1, NG - 1))
    for v in range(4 * NG):
        steps += post(B - 1, v)
    return steps


def post(b, v):
    return {
        1: [("yturn", b, NG - 1), ("ynorm", b, NG - 1)],
        2: [("pturn", b, 0)], 3: [("proj", b, 0)], 4: [("pturn", b, 1)], 5: [("proj", b, 1)],
        6: [("ln2", b)], 7: [("gturn", b, 0)], 8: [("gate", b, 0)], 9: [("gturn", b, 1)], 10: [("gate", b, 1)],
        11: [("top2", b)], 12: [("rank", b)], 13: [("send", b)],
    }.get(v, [])


def build(nc, x, ctx_in, g_xattn, g_ffn, wp, bp, wg, w1, w2, w3, cst, pad, out, xs, yt):
    steps = schedule()
    pm_use = {}
    for step in steps:
        if step[0] in ("mrow", "yturn", "pturn", "proj", "gturn", "gate", "rank"):
            pm_use[step] = len(pm_use) + 1
    with ExitStack() as stack:
        def sb(name, shape, dt=F32):
            return stack.enter_context(nc.sbuf_tensor(name, shape, dt))

        def bank(name, n=1):
            return stack.enter_context(nc.psum_tensor(name, [P, 512 * n], F32))

        def sem(name):
            return stack.enter_context(nc.semaphore(name))

        CF, CB = sb("CF", [P, NCF]), sb("CB", [P, NCB], BF16)
        X = sb("X", [P, NT, D])
        C = sb("C", [P, 2, TPB, D])
        VA = sb("VA", [P, 2, TPB, H, 2 * HD])
        SK = sb("SK", [P, STACK_BUFS, H, 6, HD], BF16)
        RES = sb("RES", [P, D])
        XN = sb("XN", [P, 2, D])
        QS = sb("QS", [P, 2, H, T], BF16)
        KS = sb("KS", [P, 2, H, T], BF16)
        PR = sb("PR", [P, P_BUFS, GROUP, 2 * P])
        W1 = sb("W1", [P, E, DB, FI])
        WP, WG, BT = sb("WP", [P, DB, D]), sb("WG", [P, DB, E]), sb("BT", [P, D])
        YS = sb("YS", [P, T])
        YN = sb("YN", [P, 2, TPB, D])
        YR = sb("YR", [P, TPB, GROUP])
        TS = sb("TS", [P, 2, DB, P])
        XR = sb("XR", [P, TPB, TOPK, ROW])
        PAD = sb("PAD", [P, E, ROW])
        ST1, MV = sb("ST1", [P, TPB, 6]), sb("MV", [P, B, TPB, 2])
        ST2, MV2 = sb("ST2", [P, TPB, 6]), sb("MV2", [P, TPB, 2])
        VE, RS, HALF = sb("VE", [P, 2, TPB]), sb("RS", [P, B, TPB]), sb("HALF", [P, TPB])
        VE2, RS2 = sb("VE2", [P, TPB]), sb("RS2", [P, TPB])
        GT = sb("GT", [P, 2])
        TG = sb("TG", [P, 2])
        MX, MR = sb("MX", [P, 2, TPB, H]), sb("MR", [P, TPB, H])
        MS = sb("MS", [P, TPB, 3, H], BF16)
        MT = sb("MT", [3 * H, 2, T], BF16)
        SC = sb("SC", [P, TPB, E])
        M8, I8 = sb("M8", [P, TPB, 8]), sb("I8", [P, TPB, 8], U32)
        IDF = sb("IDF", [P, TPB, TOPK])
        OH = sb("OH", [P, TOPK, TPB, E])
        PICK = sb("PICK", [P, TPB, E])
        AB, AC = sb("AB", [P, TPB, E], BF16), sb("AC", [P, TPB + 1, E], BF16)
        DF = sb("DF", [P, TPB])
        EX = sb("EX", [P, TPB])
        G2 = sb("G2", [P, TPB, TOPK])
        SLOT, HIT = sb("SLOT", [P, TPB, E]), sb("HIT", [P, TPB, E])
        POSF, POS = sb("POSF", [P, TPB, TOPK]), sb("POS", [P, TPB, TOPK], U32)
        PPF, PPOS = sb("PPF", [P, E]), sb("PPOS", [P, E], U32)
        CNT, TIL, END = sb("CNT", [P, E]), sb("TIL", [P, E], I32), sb("END", [P, E])
        TILF, ONE8 = sb("TILF", [P, E]), sb("ONE8", [P, E])
        PAST, BEF = sb("PAST", [1, NTILES, E]), sb("BEF", [1, NTILES, E])
        TE, TB, TR = sb("TE", [1, NTILES]), sb("TB", [1, NTILES]), sb("TR", [1, NTILES])
        TX = sb("TX", [1, 2, NTILES], I32)
        DI = sb("DI", [P, 4], U32)

        W2 = KS[:, :, :, :].rearrange("p a h t -> p (a h t)").bitcast(F32).rearrange(
            "p (e b i) -> p e b i", e=E, b=DB)
        W3 = QS[:, :, :, :].rearrange("p a h t -> p (a h t)").bitcast(F32).rearrange(
            "p (e b i) -> p e b i", e=E, b=FB)
        arena = VA[:, :, :, :, :].rearrange("p a t h c -> p (a t h c)")
        SIL = arena[:, 0:2 * FI].rearrange("p (n i) -> p n i", n=2)
        HH = arena[:, 2 * FI:4 * FI].rearrange("p (n i) -> p n i", n=2)
        HT = arena[:, 4 * FI:6 * FI].rearrange("p (n b t) -> p n b t", n=2, b=FB)
        XT = arena[:, 6 * FI:6 * FI + 2 * D].rearrange("p (n b t) -> p n b t", n=2, b=DB)
        arena2 = PR[:, :, :, :].rearrange("p a h t -> p (a h t)")
        XI = arena2[:, 0:4 * ROW].rearrange("p (n r) -> p n r", n=4)
        YO = arena2[:, 4 * ROW:4 * ROW + 4 * D].rearrange("p (n d) -> p n d", n=4)
        YC = C[:, :, :, :].rearrange("p a t d -> p (a t d)").rearrange("p (n k d) -> p n k d", n=4, k=TOPK)

        PT = [bank("PT0"), bank("PT1")]
        PS = [bank("PS0"), bank("PS1")]
        PK = [bank("PK0"), bank("PK1")]
        PY = bank("PY")
        PM = bank("PM")
        P1, P2 = [PT[0], PS[0]], [PT[1], PS[1]]
        PHT, PXT, PYO = PK, PM, PY

        const_in = sem("const_in")
        x_in = [sem(f"x_in{b}") for b in range(B)]
        ctx_in_ready = [sem(f"ctx_in{b}") for b in range(B)]
        small_in, w1_in, w2_in, w3_in, pad_in, spare_out = (sem(n) for n in (
            "small_in", "w1_in", "w2_in", "w3_in", "pad_in", "spare_out"))
        setup_done, tanh_done, bias_done = sem("setup_done"), sem("tanh_done"), sem("bias_done")
        pool_step, dve_step, act_step = sem("pool_step"), sem("dve_step"), sem("act_step")
        var_ready, rstd_ready, var2_ready, rstd2_ready = (sem(n) for n in (
            "var_ready", "rstd_ready", "var2_ready", "rstd2_ready"))
        xn_ready, stack_ready, stack_turned = sem("xn_ready"), sem("stack_ready"), sem("stack_turned")
        parts_act, parts_dve = sem("parts_act"), sem("parts_dve")
        s_ready, max_taken = sem("s_ready"), sem("max_taken")
        mrow_ready = sem("mrow_ready")
        mrow_in = [sem("mrow_in0"), sem("mrow_in1")]
        k_ready, exp_ready, pv_done = sem("k_ready"), sem("exp_ready"), sem("pv_done")
        y_out = sem("y_out")
        pm_full, pm_free = sem("pm_full"), sem("pm_free")
        xn2_ready, sel_ready, pos_ready, sent = sem("xn2_ready"), sem("sel_ready"), sem("pos_ready"), sem("sent")
        rows_copied = sem("rows_copied")
        diff_ready, ediff_ready = sem("diff_ready"), sem("ediff_ready")
        table_ready, tile_admitted = sem("table_ready"), sem("tile_admitted")
        xi_in = [sem(f"xi_in{i}") for i in range(4)]
        f_xt, f_xts, f_h1, f_sil, f_h2, f_h, f_ht, f_hts, f_y, f_yo, f_dest = (sem(n) for n in (
            "f_xt", "f_xts", "f_h1", "f_sil", "f_h2", "f_h", "f_ht", "f_hts", "f_y", "f_yo", "f_dest"))
        f_sent = [sem(f"f_sent{i}") for i in range(4)]
        yc_in = [sem(f"yc_in{i}") for i in range(4)]
        sum_ready, out_done = sem("sum_ready"), sem("out_done")

        ident = CF[:, C_ID:C_ID + P]
        ident_b = CB[:, C_ID:C_ID + P]
        block = stack.enter_context(nc.Block())

        def keys_of(t, j):
            lo = P * t + QUAD * j - WINDOW
            return max(0, -lo), min(BAND, T - lo), lo

        def queries_of(kt):
            lo, hi = max(0, P * kt - WINDOW), min(T, P * kt + P + WINDOW)
            return lo, hi, lo - (P * kt - WINDOW)

        @block.sync
        def _(sp):
            sp.dma_start(C[:, 0, :, :], ctx_in[0:T, :].rearrange("(t p) d -> p t d", p=P)).then_inc(ctx_in_ready[0], 16)
            sp.dma_start(X[:, 0:TPB, :], x[0:T, :].rearrange("(t p) d -> p t d", p=P)).then_inc(x_in[0], 16)
            sp.dma_start(CF[:, :], cst[:, :]).then_inc(const_in, 16)
            sp.dma_start(GT[:, 0:1], g_xattn.partition_broadcast(P)).then_inc(small_in, 16)
            sp.dma_start(GT[:, 1:2], g_ffn.partition_broadcast(P)).then_inc(small_in, 16)
            sp.dma_start(BT[:, :], bp.partition_broadcast(P)).then_inc(small_in, 16)
            sp.dma_start(WP[:, :, :], wp).then_inc(small_in, 16)
            sp.dma_start(WG[:, :, :], wg).then_inc(small_in, 16)
            for b in range(1, B):
                if b == 2:
                    sp.dma_start(W1[:, :, :, :], w1).then_inc(w1_in, 16)
                    sp.dma_start(PAD[:, :, :], pad[0:E].rearrange("e p r -> p e r")).then_inc(pad_in, 16)
                    sp.dma_start(xs[E * REGION:E * REGION + SPARE * P, :],
                                 pad[E:E + SPARE].rearrange("e p r -> (e p) r")).then_inc(spare_out, 16)
                sp.dma_start(X[:, b * TPB:(b + 1) * TPB, :],
                             x[b * T:(b + 1) * T, :].rearrange("(t p) d -> p t d", p=P)).then_inc(x_in[b], 16)
                if b < 2:
                    sp.dma_start(C[:, b, :, :],
                                 ctx_in[b * T:(b + 1) * T, :].rearrange("(t p) d -> p t d", p=P)).then_inc(ctx_in_ready[b], 16)
            for step in steps:
                if step[0] == "mrow":
                    b = step[1]
                    sp.wait_ge(pm_free, pm_use[step])
                    if b >= 2:
                        sp.wait_ge(k_ready, 32 * (b - 1))
                    for part in range(3):
                        sp.dma_start(QS[PARTS + part:PARTS + part + 1, b % 2, :, :],
                                     MT[part * H:(part + 1) * H, b % 2, :]).then_inc(mrow_in[b % 2], 16)
                    if b + 2 < B:
                        sp.wait_ge(stack_ready, 8 * (b + 1))
                        sp.dma_start(C[:, b % 2, :, :], ctx_in[(b + 2) * T:(b + 3) * T, :].rearrange(
                            "(t p) d -> p t d", p=P)).then_inc(ctx_in_ready[b + 2], 16)
            sp.wait_ge(k_ready, 32 * (B - 1))
            half = E // 2
            sp.dma_start(W2[:, 0:half], w2[:, 0:half]).then_inc(w2_in, 16)
            sp.dma_start(W3[:, 0:half], w3[:, 0:half]).then_inc(w3_in, 16)
            sp.wait_ge(k_ready, 32 * B)
            sp.dma_start(W2[:, half:E], w2[:, half:E]).then_inc(w2_in, 16)
            sp.dma_start(W3[:, half:E], w3[:, half:E]).then_inc(w3_in, 16)
            sp.wait_ge(table_ready, 1)
            sp.wait_ge(sent, 16 * (NT * TOPK + E))
            sp.wait_ge(spare_out, 16)

            def load(j, r):
                row = sp.value_load(TX[0:1, 0, bass.ds(j, 1)], min_val=0, max_val=(E * REGION + (SPARE - 1) * P))
                sp.dma_start(XI[:, r, :], xs[bass.ds(row, P), :]).then_inc(xi_in[r], 16)

            def reload(j, r):
                sp.wait_ge(f_dest, j - 3)
                sp.wait_ge(f_yo, j - 3)
                load(j, r)

            for j in range(4):
                load(j, j)
            with sp.Fori(1, NTILES // 4) as i:
                for r in range(4):
                    reload(4 * i + r, r)
            for j in range(NTILES // 4 * 4, NTILES):
                reload(j, j % 4)
            for r in range(4):
                sp.wait_ge(f_sent[r], 16 * ((NTILES - r + 3) // 4))
            for t in range(NT):
                if t >= 4:
                    sp.wait_ge(sum_ready, t - 3)
                sp.dma_start(YC[:, t % 4, :, :], yt[t * P * TOPK:(t + 1) * P * TOPK, :].rearrange(
                    "(p k) d -> p k d", k=TOPK)).then_inc(yc_in[t % 4], 16)
            sp.wait_ge(out_done, 16 * NT)

        @block.gpsimd
        def _(pool):
            done = [0]

            def chain(ins):
                done[0] += 1
                ins.then_inc(pool_step, 1)
                pool.wait_ge(pool_step, done[0])

            pool.memset(HALF[:, :], -0.5).then_inc(setup_done, 1)
            pool.wait_ge(setup_done, 1)
            pool.memset(KS[PARTS:ROWS, :, :, :], 1.0).then_inc(setup_done, 1)
            pool.wait_ge(setup_done, 2)
            pool.memset(VA[:, :, :, :, HD:2 * HD], 1.0).then_inc(setup_done, 1)
            pool.memset(AC[:, 0, :], 0.0).then_inc(setup_done, 1)
            pool.memset(ONE8[:, :], 1.0).then_inc(setup_done, 1)
            pool.wait_ge(setup_done, 5)
            for step in steps:
                kind = step[0]
                if kind == "ln1":
                    b = step[1]
                    pool.wait_ge(var_ready, b + 1)
                    pool.tensor_tensor(RS[:, b, :], VE[:, b % 2, :], HALF[:, :], ALU.pow).then_inc(rstd_ready, 1)
                elif kind == "prep":
                    n = step[1]
                    b, t, side = n // 8, n % 8 // 2, n % 2
                    buf = SK[:, n % STACK_BUFS]
                    if n >= STACK_BUFS:
                        pool.wait_ge(stack_turned, 2 * (n - STACK_BUFS + 1))
                    if side == 0:
                        if t == 0:
                            pool.wait_ge(ctx_in_ready[b], 16)
                        src = C[:, b % 2, t, :]
                        one, two, three = slice(0, 3), slice(3, 6, 2), 4
                    else:
                        pool.wait_ge(xn_ready, 4 * b + t + 1)
                        src = XN[:, (4 * b + t) % 2, :]
                        one, two, three = slice(2, 5), slice(1, 6, 4), 0
                    src = src.rearrange("p (h c) -> p h c", h=H)
                    res = RES[:, :].rearrange("p (h c) -> p h c", h=H)
                    chain(pool.tensor_copy(buf[:, :, one, :], src.unsqueeze(2).to_broadcast([P, H, 3, HD])))
                    chain(pool.tensor_tensor(res, src, buf[:, :, one.start, :], ALU.subtract))
                    chain(pool.tensor_copy(buf[:, :, two, :], res.unsqueeze(2).to_broadcast([P, H, 2, HD])))
                    pool.tensor_tensor(buf[:, :, three, :], res, buf[:, :, two.start, :],
                                       ALU.subtract).then_inc(stack_ready, 1)
                    pool.wait_ge(stack_ready, n + 1)
                    if side == 0:
                        if b >= 2:
                            pool.wait_ge(pv_done, 16 * (b - 1))
                        pool.tensor_copy(VA[:, b % 2, t, :, 0:HD], src).then_inc(setup_done, 1)
                        pool.wait_ge(setup_done, 6 + 4 * b + t)
                    else:
                        if n == 1:
                            pool.wait_ge(bias_done, 1)
                        xt = X[:, 4 * b + t, :]
                        chain(pool.tensor_tensor(xt, xt, BT[:, :], ALU.add))
                elif kind == "ln2":
                    b = step[1]
                    pool.wait_ge(var2_ready, b + 1)
                    pool.tensor_tensor(RS2[:, :], VE2[:, :], HALF[:, :], ALU.pow).then_inc(rstd2_ready, 1)
                    for t in range(TPB):
                        pool.wait_ge(xn2_ready, 4 * b + t + 1)
                        pool.tensor_copy(XR[:, t, 1, 0:D], XR[:, t, 0, 0:D]).then_inc(rows_copied, 1)
                elif kind == "send":
                    b = step[1]
                    pool.wait_ge(pos_ready, b + 1)
                    pool.wait_ge(rows_copied, 4 * (b + 1))
                    for t in range(TPB):
                        for k in range(TOPK):
                            pool.indirect_dma_start(
                                xs[:, :], bass.IndirectOffsetOnAxis(POS[:, t, k:k + 1], 0),
                                XR[:, t, k, :], None).then_inc(sent, 16)
            pool.wait_ge(pad_in, 16)
            pool.wait_ge(table_ready, 1)
            for e in range(E):
                pool.indirect_dma_start(xs[:, :], bass.IndirectOffsetOnAxis(PPOS[:, e:e + 1], 0),
                                        PAD[:, e, :], None).then_inc(sent, 16)

            def scatter(j, r):
                pool.wait_ge(f_dest, j + 1)
                pool.wait_ge(f_yo, j + 1)
                pool.sem_inc(tile_admitted, 1)
                pool.indirect_dma_start(yt[:, :], bass.IndirectOffsetOnAxis(DI[:, r:r + 1], 0),
                                        YO[:, r, :], None).then_inc(f_sent[r], 16)

            with pool.Fori(0, NTILES // 4) as i:
                for r in range(4):
                    scatter(4 * i + r, r)
            for r in range(NTILES % 4):
                scatter(NTILES // 4 * 4 + r, r)

        @block.scalar
        def _(act):
            act.wait_ge(small_in, 16 * 5)
            nc.scalar.activation(TG[:, :], GT[:, :], ACT.Tanh).then_inc(tanh_done, 1)
            for step in steps:
                kind = step[0]
                if kind == "prep":
                    n = step[1]
                    b, t, side = n // 8, n % 8 // 2, n % 2
                    dst = (KS, QS)[side]
                    act.wait_ge(stack_turned, 2 * n + 1)
                    if n % 8 == 0 and b >= 2:
                        act.wait_ge(k_ready, 32 * (b - 1))
                    nc.scalar.activation(
                        dst[0:PARTS, b % 2, 0:8, t * P:(t + 1) * P],
                        PT[0][0:PARTS, :].bitcast(BF16).rearrange("p (h t) -> p h t", h=8),
                        ACT.Copy).then_inc(parts_act, 1)
                elif kind == "score":
                    b, v = step[1:]
                    kt, n = v % 4, 16 * b + v
                    lo, hi, _ = queries_of(kt)
                    w = hi - lo
                    if n >= P_BUFS:
                        act.wait_ge(pv_done, n - P_BUFS + 1)
                    for pair in range(2):
                        act.wait_ge(k_ready, 2 * n + pair + 1)
                        nc.scalar.activation(
                            PR[:, n % P_BUFS, 2 * pair:2 * pair + 2, 0:w],
                            PK[pair][:, 0:2 * w].rearrange("p (h q) -> p h q", h=2),
                            ACT.Exp).then_inc(exp_ready, 1)
                elif kind == "yout":
                    b, g = step[1:]
                    act.wait_ge(pv_done, 16 * b + 4 * g + 4)
                    if b + g > 0:
                        before = 4 * b + g - 1
                        act.wait_ge(pm_free, pm_use["yturn", before // NG, before % NG])
                    nc.scalar.activation(YS[:, :], PY[:, :], ACT.Copy).then_inc(y_out, 1)
                elif kind == "top2":
                    b = step[1]
                    act.wait_ge(diff_ready, b + 1)
                    nc.scalar.activation(EX[:, :], DF[:, :], ACT.Exp).then_inc(ediff_ready, 1)

            def turn_x(j, r):
                act.wait_ge(f_xt, j + 1)
                nc.scalar.activation(XT[:, r % 2, :, :], PXT[:, 0:D].rearrange("p (b t) -> p b t", b=DB),
                                     ACT.Copy).then_inc(f_xts, 1)

            def silu(j, r):
                act.wait_ge(f_h1, j + 1)
                nc.scalar.activation(SIL[:, r % 2, :], P1[r % 2][:, :], ACT.Silu).then_inc(f_sil, 1)

            turn_x(0, 0)
            turn_x(1, 1)
            silu(0, 0)
            with act.Fori(0, (NTILES - 3) // 2) as i:
                for r in range(2):
                    j = 2 * i + r
                    act.wait_ge(f_h, j + 1)
                    silu(j + 1, r + 1)
                    turn_x(j + 2, r)
            j = NTILES - 3
            act.wait_ge(f_h, j + 1)
            silu(j + 1, j + 1)
            turn_x(j + 2, j)
            act.wait_ge(f_h, j + 2)
            silu(j + 2, j + 2)
            for t in range(NT):
                act.wait_ge(sum_ready, t + 1)
                act.dma_start(out[t * P:(t + 1) * P, :], X[:, t, :]).then_inc(out_done, 16)

        @block.vector
        def _(dve):
            done = [0]
            use = [0]

            def chain(ins):
                done[0] += 1
                ins.then_inc(dve_step, 1)
                dve.wait_ge(dve_step, done[0])

            def pm_used():
                use[0] += 1
                dve.wait_ge(pm_full, use[0])

            dve.wait_ge(const_in, 16)
            chain(nc.vector.tensor_copy(CB[:, :], CF[:, 0:NCB]))
            for step in steps:
                kind = step[0]
                if kind == "ln1":
                    b = step[1]
                    dve.wait_ge(x_in[b], 16)
                    for t in range(TPB):
                        last = nc.vector.bn_stats(ST1[:, t, :], X[:, 4 * b + t, :])
                    chain(last)
                    for t in range(TPB):
                        last = nc.vector.bn_aggr(MV[:, b, t, :], ST1[:, t, :])
                    chain(last)
                    nc.vector.tensor_scalar(VE[:, b % 2, :], MV[:, b, :, 1], EPS, None, ALU.add).then_inc(var_ready, 1)
                    dve.wait_ge(rstd_ready, b + 1)
                    chain(nc.vector.tensor_scalar(RS[:, b, :], RS[:, b, :], Q_SCALE, None, ALU.mult))
                    if b == 0:
                        dve.wait_ge(tanh_done, 1)
                        nc.vector.tensor_scalar(BT[:, :], BT[:, :], TG[:, 0:1], None, ALU.mult).then_inc(bias_done, 1)
                elif kind == "prep":
                    n = step[1]
                    b, t, side = n // 8, n % 8 // 2, n % 2
                    if side == 0:
                        i = 4 * b + t
                        if i >= 2:
                            dve.wait_ge(stack_ready, 2 * i - 2)
                        nc.vector.tensor_scalar(XN[:, i % 2, :], X[:, i, :], MV[:, b, t, 0:1], RS[:, b, t:t + 1],
                                                ALU.subtract, ALU.mult).then_inc(xn_ready, 1)
                    dst = (KS, QS)[side]
                    dve.wait_ge(stack_turned, 2 * n + 2)
                    if n % 8 == 0 and b >= 2:
                        dve.wait_ge(k_ready, 32 * (b - 1))
                    nc.vector.tensor_copy(
                        dst[0:PARTS, b % 2, 8:16, t * P:(t + 1) * P],
                        PT[1][0:PARTS, :].bitcast(BF16).rearrange("p (h t) -> p h t", h=8)).then_inc(parts_dve, 1)
                elif kind == "smax":
                    b, t, half = step[1:]
                    for u in range(3 * half, 3 * half + 3):
                        i = NS * (4 * b + t) + u
                        h0, nh = SHEADS[u]
                        dve.wait_ge(s_ready, i + 1)
                        nc.vector.tensor_reduce(
                            MX[:, b % 2, t, h0:h0 + nh],
                            PS[i % 2][:, 0:nh * BAND].rearrange("p (h c) -> p h c", h=nh),
                            AX.X, ALU.max).then_inc(max_taken, 1)
                elif kind == "mrow":
                    b = step[1]
                    m = MX[:, b % 2, :, :]
                    dve.wait_ge(max_taken, NS * 4 * (b + 1))
                    chain(nc.vector.tensor_scalar(MS[:, :, 0, :], m, -1.0, None, ALU.mult))
                    chain(nc.vector.scalar_tensor_tensor(out=MR[:, :, :], in0=m, scalar=-1.0, in1=MS[:, :, 0, :],
                                                         op0=ALU.mult, op1=ALU.subtract))
                    chain(nc.vector.tensor_copy(MS[:, :, 1, :], MR[:, :, :]))
                    nc.vector.tensor_tensor(MS[:, :, 2, :], MR[:, :, :], MS[:, :, 1, :],
                                            ALU.subtract).then_inc(mrow_ready, 1)
                    pm_used()
                    if b >= 2:
                        dve.wait_ge(mrow_in[b % 2], 48)
                    nc.vector.tensor_copy(MT[:, b % 2, :], PM[0:3 * H, 0:T // 2].bitcast(BF16)
                                          ).then_inc(pm_free, 1)
                elif kind == "ynorm":
                    b, g = step[1:]
                    pm_used()
                    y = PM[:, :].rearrange("p (t h c) -> p t h c", t=TPB, h=GROUP)
                    chain(nc.vector.reciprocal(YR[:, :, :], y[:, :, :, HD]))
                    nc.vector.tensor_tensor(
                        YN[:, b % 2, :, g * 64:(g + 1) * 64].rearrange("p t (h c) -> p t h c", h=GROUP),
                        y[:, :, :, 0:HD], YR[:, :, :].unsqueeze(3).to_broadcast([P, TPB, GROUP, HD]),
                        ALU.mult).then_inc(pm_free, 1)
                elif kind in ("pturn", "gturn"):
                    pm_used()
                    nc.vector.tensor_copy(TS[:, :, :, :], PM[:, :].rearrange("p (t b q) -> p t b q", t=2, b=DB)
                                          ).then_inc(pm_free, 1)
                elif kind == "proj":
                    b, half = step[1:]
                    i = 4 * b + 2 * half
                    pm_used()
                    nc.vector.scalar_tensor_tensor(
                        out=X[:, i:i + 2, :], in0=PM[:, :].rearrange("p (t d) -> p t d", t=2), scalar=TG[:, 0:1],
                        in1=X[:, i:i + 2, :], op0=ALU.mult, op1=ALU.add).then_inc(pm_free, 1)
                    dve.wait_ge(pm_free, use[0])
                elif kind == "ln2":
                    b = step[1]
                    for t in range(TPB):
                        last = nc.vector.bn_stats(ST2[:, t, :], X[:, 4 * b + t, :])
                    chain(last)
                    for t in range(TPB):
                        last = nc.vector.bn_aggr(MV2[:, t, :], ST2[:, t, :])
                    chain(last)
                    nc.vector.tensor_scalar(VE2[:, :], MV2[:, :, 1], EPS, None, ALU.add).then_inc(var2_ready, 1)
                    dve.wait_ge(rstd2_ready, b + 1)
                    if b >= 1:
                        dve.wait_ge(sent, 16 * TOPK * TPB * b)
                    for t in range(TPB):
                        nc.vector.tensor_scalar(XR[:, t, 0, 0:D], X[:, 4 * b + t, :], MV2[:, t, 0:1],
                                                RS2[:, t:t + 1], ALU.subtract, ALU.mult).then_inc(xn2_ready, 1)
                elif kind == "gate":
                    b, half = step[1:]
                    pm_used()
                    nc.vector.tensor_copy(SC[:, 2 * half:2 * half + 2, :],
                                          PM[:, 0:2 * E].rearrange("p (t e) -> p t e", t=2)).then_inc(pm_free, 1)
                    dve.wait_ge(pm_free, use[0])
                elif kind == "top2":
                    b = step[1]
                    for t in range(TPB):
                        last = nc.vector.max(M8[:, t, :], SC[:, t, :])
                    chain(last)
                    for t in range(TPB):
                        last = nc.vector.max_index(I8[:, t, :], M8[:, t, :], SC[:, t, :])
                    chain(last)
                    nc.vector.tensor_tensor(DF[:, :], M8[:, :, 1], M8[:, :, 0], ALU.subtract).then_inc(diff_ready, 1)
                    chain(nc.vector.tensor_copy(IDF[:, :, :], I8[:, :, 0:TOPK]))
                    iota = CF[:, C_IOTA:C_IOTA + E].unsqueeze(1).to_broadcast([P, TPB, E])
                    for k in range(TOPK):
                        last = nc.vector.tensor_tensor(
                            OH[:, k, :, :], iota, IDF[:, :, k].unsqueeze(2).to_broadcast([P, TPB, E]), ALU.is_equal)
                    chain(last)
                    chain(nc.vector.tensor_tensor(AB[:, :, :], OH[:, 0, :, :], OH[:, 1, :, :], ALU.add))
                    if b >= 1:
                        chain(nc.vector.tensor_copy(AC[:, 0, :], AC[:, TPB, :]))
                    else:
                        dve.wait_ge(setup_done, 5)
                    for t in range(TPB):
                        last = nc.vector.tensor_tensor(AC[:, t + 1, :], AC[:, t, :], AB[:, t, :], ALU.add)
                        if t < TPB - 1:
                            chain(last)
                    last.then_inc(sel_ready, 1)
                    dve.wait_ge(ediff_ready, b + 1)
                    chain(nc.vector.tensor_scalar(DF[:, :], EX[:, :], 1.0, None, ALU.add))
                    chain(nc.vector.reciprocal(G2[:, :, 0], DF[:, :]))
                    chain(nc.vector.tensor_tensor(G2[:, :, 1], G2[:, :, 0], EX[:, :], ALU.mult))
                    chain(nc.vector.tensor_scalar(XR[:, :, :, D + 1], G2[:, :, :], TG[:, 1:2], None, ALU.mult))
                    for k in range(TOPK):
                        last = nc.vector.tensor_scalar(XR[:, :, k, D], CF[:, C_DEST + 4 * b:C_DEST + 4 * b + 4],
                                                       float(k), None, ALU.add)
                    chain(last)
                elif kind == "rank":
                    b = step[1]
                    pm_used()
                    reg = CF[:, C_REG:C_REG + E].unsqueeze(1).to_broadcast([P, TPB, E])
                    if b == B - 1:
                        chain(nc.vector.tensor_copy(CNT[:, :], PM[:, TPB * E:TPB * E + E]))
                    nc.vector.tensor_tensor(SLOT[:, :, :], PM[:, 0:TPB * E].rearrange("p (t e) -> p t e", t=TPB),
                                            reg, ALU.add).then_inc(pm_free, 1)
                    dve.wait_ge(pm_free, use[0])
                    for k in range(TOPK):
                        chain(nc.vector.tensor_tensor(HIT[:, :, :], OH[:, k, :, :], SLOT[:, :, :], ALU.mult))
                        chain(nc.vector.tensor_reduce(POSF[:, :, k], HIT[:, :, :], AX.X, ALU.add))
                    if b >= 1:
                        dve.wait_ge(sent, 16 * TOPK * TPB * b)
                    nc.vector.tensor_copy(POS[:, :, :], POSF[:, :, :]).then_inc(pos_ready, 1)
            chain(nc.vector.tensor_tensor(PPF[:, :], CNT[:, :], CF[:, C_REG:C_REG + E], ALU.add))
            chain(nc.vector.tensor_scalar(PPOS[:, :], PPF[:, :], CF[:, C_P:C_P + 1], None, ALU.add))
            chain(nc.vector.tensor_scalar(TIL[:, :], CNT[:, :], 1.0 / P, (P - 1) / P - (P - 1) / (2 * P),
                                          ALU.mult, ALU.add))
            chain(nc.vector.tensor_copy(TILF[:, :], TIL[:, :]))
            chain(nc.vector.tensor_tensor_scan(END[:, :], ONE8[:, :], TILF[:, :], 0.0, ALU.mult, ALU.add))
            chain(nc.vector.tensor_tensor(
                PAST[:, :, :], CF[0:1, C_TILE:C_TILE + NTILES].unsqueeze(2).to_broadcast([1, NTILES, E]),
                END[0:1, :].unsqueeze(1).to_broadcast([1, NTILES, E]), ALU.is_ge))
            chain(nc.vector.tensor_reduce(TE[:, :], PAST[:, :, :], AX.X, ALU.add))
            chain(nc.vector.tensor_tensor(BEF[:, :, :], PAST[:, :, :],
                                          TILF[0:1, :].unsqueeze(1).to_broadcast([1, NTILES, E]), ALU.mult))
            chain(nc.vector.tensor_reduce(TB[:, :], BEF[:, :, :], AX.X, ALU.add))
            chain(nc.vector.tensor_tensor(TB[:, :], CF[0:1, C_TILE:C_TILE + NTILES], TB[:, :], ALU.subtract))
            chain(nc.vector.tensor_scalar(TB[:, :], TB[:, :], float(P), None, ALU.mult))
            chain(nc.vector.scalar_tensor_tensor(out=TR[:, :], in0=TE[:, :], scalar=float(REGION), in1=TB[:, :],
                                                 op0=ALU.mult, op1=ALU.add))
            chain(nc.vector.tensor_copy(TX[:, 0, :], TR[:, :]))
            nc.vector.tensor_scalar(TX[:, 1, :], TE[:, :], float(E - 1), None, ALU.min).then_inc(table_ready, 1)

            def product(j, r):
                dve.wait_ge(f_sil, j + 1)
                dve.wait_ge(f_h2, j + 1)
                nc.vector.tensor_tensor(HH[:, r % 2, :], SIL[:, r % 2, :], P2[r % 2][:, :], ALU.mult).then_inc(f_h, 1)

            def turn_h(j, r):
                dve.wait_ge(f_ht, j + 1)
                nc.vector.tensor_copy(HT[:, r % 2, :, :],
                                      PHT[r % 2][:, :].rearrange("p (b t) -> p b t", b=FB)).then_inc(f_hts, 1)

            def gated(j, r):
                dve.wait_ge(xi_in[r], xin(j, r))
                nc.vector.tensor_copy(DI[:, r:r + 1], XI[:, r, D:D + 1]).then_inc(f_dest, 1)
                dve.wait_ge(f_y, j + 1)
                nc.vector.tensor_scalar(YO[:, r, :], PYO[:, 0:D], XI[:, r, D + 1:D + 2], None,
                                        ALU.mult).then_inc(f_yo, 1)

            def xin(j, r):
                return 4 * (j - r) + 16

            def step_of(j, r, wait_sent):
                turn_h(j, r)
                product(j + 1, r + 1)
                if wait_sent:
                    dve.wait_ge(f_sent[r % 4], 4 * (j - r % 4))
                gated(j, r % 4)

            product(0, 0)
            for j in range(4):
                step_of(j, j, False)
            with dve.Fori(1, (NTILES - 3) // 4) as i:
                for r in range(4):
                    step_of(4 * i + r, r, True)
            for j in range((NTILES - 3) // 4 * 4, NTILES - 1):
                step_of(j, j % 4, True)
            j = NTILES - 1
            turn_h(j, j)
            dve.wait_ge(f_sent[j % 4], 4 * (j - j % 4))
            gated(j, j % 4)
            for t in range(NT):
                dve.wait_ge(yc_in[t % 4], 16 * (t // 4 + 1))
                chain(nc.vector.tensor_tensor(X[:, t, :], X[:, t, :], YC[:, t % 4, 0, :], ALU.add))
                nc.vector.tensor_tensor(X[:, t, :], X[:, t, :], YC[:, t % 4, 1, :], ALU.add).then_inc(sum_ready, 1)

        @block.tensor
        def _(pe):
            use = [0]

            def pm_take():
                if use[0]:
                    pe.wait_ge(pm_free, use[0])
                use[0] += 1

            pe.wait_ge(dve_step, 1)
            pe.wait_ge(setup_done, 5)
            pe.wait_ge(small_in, 16 * 5)
            for step in steps:
                kind = step[0]
                if kind == "prep":
                    n = step[1]
                    pe.wait_ge(stack_ready, n + 1)
                    for half in range(2):
                        if n >= 1:
                            pe.wait_ge((parts_act, parts_dve)[half], n)
                        for h in range(8):
                            last = nc.tensor.transpose(
                                PT[half][0:PARTS, 64 * h:64 * (h + 1)].bitcast(BF16),
                                SK[:, n % STACK_BUFS, 8 * half + h, :, :].rearrange("p s c -> p (s c)"), ident_b)
                        last.then_inc(stack_turned, 1)
                elif kind == "smax":
                    b, t, half = step[1:]
                    if t == 0 and half == 0:
                        pe.wait_ge(parts_act, 8 * (b + 1))
                        pe.wait_ge(parts_dve, 8 * (b + 1))
                    mask = CB[:, C_MS + BAND * (0 if t == 0 else 2 if t == TPB - 1 else 1):][:, 0:BAND]
                    left = 2 * QUAD if t == 0 else QUAD
                    right = BAND - (2 * QUAD if t == TPB - 1 else QUAD)
                    for u in range(3 * half, 3 * half + 3):
                        i = NS * (4 * b + t) + u
                        h0, nh = SHEADS[u]
                        if i >= 2:
                            pe.wait_ge(max_taken, i - 1)
                        s = PS[i % 2][:, 0:nh * BAND].rearrange("p (h c) -> p h c", h=nh)
                        for n, (c0, c1) in enumerate(((0, left), (right, BAND))):
                            nc.tensor.matmul(s[:, :, c0:c1], ident_b,
                                             mask[:, c0:c1].unsqueeze(1).to_broadcast([P, nh, c1 - c0]),
                                             start=(n == 0), stop=False, skip_group_check=True)
                        for h in range(nh):
                            for j in range(P // QUAD):
                                c0, c1, lo = keys_of(t, j)
                                q0 = t * P + QUAD * j
                                last = nc.tensor.matmul(s[QUAD * j:QUAD * (j + 1), h, c0:c1],
                                                        QS[0:PARTS, b % 2, h0 + h, q0:q0 + QUAD],
                                                        KS[0:PARTS, b % 2, h0 + h, lo + c0:lo + c1],
                                                        start=False, stop=True, skip_group_check=True)
                        last.then_inc(s_ready, 1)
                elif kind == "mrow":
                    b = step[1]
                    pe.wait_ge(mrow_ready, b + 1)
                    pm_take()
                    for t in range(TPB):
                        last = nc.tensor.transpose(PM[0:3 * H, 64 * t:64 * (t + 1)].bitcast(BF16),
                                                   MS[:, t, :, :].rearrange("p a h -> p (a h)"), ident_b)
                    last.then_inc(pm_full, 1)
                elif kind == "score":
                    b, v = step[1:]
                    g, kt, n = v // 4, v % 4, 16 * b + v
                    lo, hi, c0 = queries_of(kt)
                    w = hi - lo
                    if v == 0:
                        pe.wait_ge(mrow_in[b % 2], 48 * (b // 2 + 1))
                    for pair in range(2):
                        if n >= 1:
                            pe.wait_ge(exp_ready, 2 * n + pair - 1)
                        bank_ = PK[pair][:, 0:2 * w].rearrange("p (h q) -> p h q", h=2)
                        nc.tensor.matmul(bank_, ident_b,
                                         CB[:, C_MT + c0:C_MT + c0 + w].unsqueeze(1).to_broadcast([P, 2, w]),
                                         start=True, stop=False, skip_group_check=True)
                        for h in range(2):
                            hh = GROUP * g + 2 * pair + h
                            last = nc.tensor.matmul(bank_[:, h, :], KS[0:ROWS, b % 2, hh, kt * P:(kt + 1) * P],
                                                    QS[0:ROWS, b % 2, hh, lo:hi], start=False, stop=(h == 1),
                                                    skip_group_check=True)
                        last.then_inc(k_ready, 1)
                elif kind == "pv":
                    b, v = step[1:]
                    g, kt, n = v // 4, v % 4, 16 * b + v
                    lo, hi, _ = queries_of(kt)
                    pe.wait_ge(exp_ready, 2 * n + 2)
                    if v == 0:
                        pe.wait_ge(setup_done, 5 + 4 * (b + 1))
                    if kt == 0 and n > 0:
                        pe.wait_ge(y_out, 4 * b + g)
                    for h in range(GROUP):
                        last = nc.tensor.matmul(PY[QUAD * h:QUAD * (h + 1), lo:hi],
                                                VA[:, b % 2, kt, GROUP * g + h, :],
                                                PR[:, n % P_BUFS, h, 0:hi - lo], start=(kt == 0),
                                                stop=(kt == TPB - 1), skip_group_check=True)
                    last.then_inc(pv_done, 1)
                elif kind == "yturn":
                    b, g = step[1:]
                    pe.wait_ge(y_out, 4 * b + g + 1)
                    pm_take()
                    for t in range(TPB):
                        last = nc.tensor.transpose(PM[:, P * t:P * (t + 1)], YS[:, P * t:P * (t + 1)], ident)
                    last.then_inc(pm_full, 1)
                elif kind in ("pturn", "gturn"):
                    b, half = step[1:]
                    if kind == "pturn":
                        pe.wait_ge(pm_free, pm_use["yturn", b, NG - 1])
                    else:
                        pe.wait_ge(xn2_ready, 4 * (b + 1))
                    pm_take()
                    for t in range(2):
                        src = YN[:, b % 2, 2 * half + t, :] if kind == "pturn" else XR[:, 2 * half + t, 0, 0:D]
                        for blk in range(DB):
                            c = (t * DB + blk) * P
                            last = nc.tensor.transpose(PM[:, c:c + P], src[:, blk * P:(blk + 1) * P], ident)
                    last.then_inc(pm_full, 1)
                elif kind in ("proj", "gate"):
                    pm_take()
                    w, n = (WP, D) if kind == "proj" else (WG, E)
                    for t in range(2):
                        for blk in range(DB):
                            last = nc.tensor.matmul(PM[:, t * n:(t + 1) * n], TS[:, t, blk, :], w[:, blk, :],
                                                    start=(blk == 0), stop=(blk == DB - 1))
                    last.then_inc(pm_full, 1)
                elif kind == "rank":
                    b = step[1]
                    pe.wait_ge(sel_ready, b + 1)
                    pm_take()
                    n = TPB * E
                    nc.tensor.matmul(PM[:, 0:n], CB[:, C_UP:C_UP + P], AB[:, :, :].rearrange("p t e -> p (t e)"),
                                     start=True, stop=False, skip_group_check=True)
                    nc.tensor.matmul(PM[:, 0:n], CB[:, C_ONE:C_ONE + P],
                                     AC[:, 0:TPB, :].rearrange("p t e -> p (t e)"),
                                     start=False, stop=False, skip_group_check=True)
                    nc.tensor.matmul(PM[:, n:n + E], CB[:, C_ONE:C_ONE + P], AC[:, TPB, :],
                                     start=False, stop=True, skip_group_check=True).then_inc(pm_full, 1)

            def turn_x(j, r):
                pe.wait_ge(xi_in[r % 4], 4 * (j - r % 4) + 16)
                for blk in range(DB):
                    last = nc.tensor.transpose(PXT[:, blk * P:(blk + 1) * P], XI[:, r % 4, blk * P:(blk + 1) * P], ident)
                last.then_inc(f_xt, 1)

            def expert(j):
                return pe.value_load(TX[0:1, 1, bass.ds(j, 1)], min_val=0, max_val=E - 1)

            def hidden(w, bank_, e, r, done):
                flat = w.rearrange("p e b i -> p (e b i)")
                for blk in range(DB):
                    last = nc.tensor.matmul(bank_[:, :], XT[:, r % 2, blk, :],
                                            flat[:, bass.ds(e * (DB * FI) + blk * FI, FI)],
                                            start=(blk == 0), stop=(blk == DB - 1))
                last.then_inc(done, 1)

            def turn_h(j, r):
                pe.wait_ge(f_h, j + 1)
                for blk in range(FB):
                    last = nc.tensor.transpose(PHT[r % 2][:, blk * P:(blk + 1) * P],
                                               HH[:, r % 2, blk * P:(blk + 1) * P], ident)
                last.then_inc(f_ht, 1)

            def outputs(j, r, e):
                pe.wait_ge(f_hts, j + 1)
                pe.wait_ge(f_yo, j)
                flat = W3.rearrange("p e b i -> p (e b i)")
                for blk in range(FB):
                    last = nc.tensor.matmul(PYO[:, 0:D], HT[:, r % 2, blk, :],
                                            flat[:, bass.ds(e * (FB * D) + blk * D, D)],
                                            start=(blk == 0), stop=(blk == FB - 1))
                last.then_inc(f_y, 1)

            pe.wait_ge(pm_free, use[0])
            pe.wait_ge(table_ready, 1)
            turn_x(0, 0)
            pe.wait_ge(f_xts, 1)
            turn_x(1, 1)
            pe.wait_ge(w1_in, 16)
            pe.wait_ge(w2_in, 32)
            pe.wait_ge(w3_in, 32)
            e0 = expert(0)
            hidden(W1[:, :, :, :], P1[0], e0, 0, f_h1)
            hidden(W2, P2[0], e0, 0, f_h2)

            def steady(j, r, turn=True):
                e_next = expert(j + 1)
                pe.wait_ge(f_xts, j + 2)
                hidden(W1[:, :, :, :], P1[(r + 1) % 2], e_next, r + 1, f_h1)
                turn_h(j, r)
                if turn:
                    turn_x(j + 2, r + 2)
                hidden(W2, P2[(r + 1) % 2], e_next, r + 1, f_h2)
                outputs(j, r, expert(j))

            n = (NTILES - 3) // 4
            for j in (0, 1, 2, 3):
                steady(j, j)
            with pe.Fori(1, n) as i:
                for r in range(4):
                    steady(4 * i + r, r)
            for j in range(4 * n, NTILES - 1):
                steady(j, j % 4, turn=j + 2 < NTILES)
            j = NTILES - 1
            turn_h(j, j)
            outputs(j, j, expert(j))


_OUT = (B, T, D)


def kernel(**inputs):
    import concourse.bacc as _bacc
    from concourse.bass_utils import run_bass_kernel_spmd as _run

    a = {k: np.asarray(v) for k, v in inputs.items()}

    def rows(w, blocks):
        w = np.swapaxes(w, -1, -2)
        w = w.reshape(*w.shape[:-2], blocks, P, w.shape[-1])
        return np.ascontiguousarray(np.moveaxis(w, -2, 0))

    cst, pad = constants()
    arrays = {
        "x": np.ascontiguousarray(a["x"].reshape(NTOK, D)),
        "ctx_in": np.ascontiguousarray(a["ctx_1024"].reshape(NTOK, D)),
        "g_xattn": np.ascontiguousarray(a["g_xattn"]),
        "g_ffn": np.ascontiguousarray(a["g_ffn"]),
        "wp": rows(a["L0_xattn_W_proj"], DB),
        "bp": np.ascontiguousarray(a["L0_xattn_b_proj"]),
        "wg": rows(a["L0_ffn_Wg"], DB),
        "w1": rows(a["L0_ffn_W1"], DB),
        "w2": rows(a["L0_ffn_W2"], DB),
        "w3": rows(a["L0_ffn_W3"], FB),
        "cst": cst,
        "pad": pad,
    }
    nc = _bacc.Bacc("TRN2", target_bir_lowering=False, num_devices=1)
    args = {k: nc.dram_tensor(k, v.shape, mybir.dt.from_np(v.dtype), kind="ExternalInput").ap()
            for k, v in arrays.items()}
    out = nc.dram_tensor("out", (NTOK, D), F32, kind="ExternalOutput").ap()
    xs = nc.dram_tensor("xs", (E * REGION + SPARE * P, ROW), F32, kind="Internal").ap()
    yt = nc.dram_tensor("yt", (SLOTS + (E + SPARE) * P, D), F32, kind="Internal").ap()
    build(nc, out=out, xs=xs, yt=yt, **args)
    r = _run(nc, [arrays], core_ids=[0])
    return r.results[0]["out"].reshape(_OUT)
```

```python
from contextlib import ExitStack

import numpy as np
import concourse.bass as bass
from concourse import mybir

F32 = mybir.dt.float32
BF16 = mybir.dt.bfloat16
U32 = mybir.dt.uint32
I32 = mybir.dt.int32
ALU = mybir.AluOpType
ACT = mybir.ActivationFunctionType
AX = mybir.AxisListType

P = 128
B, T, D = 4, 512, 256
H, HD, WINDOW = 16, 16, 64
E, FI, TOPK = 8, 512, 2
NTOK = B * T
TPB = T // P
NT = NTOK // P
DB, FB = D // P, FI // P
EPS = 1e-5
Q_SCALE = 1.0 / HD ** 0.5
QUAD = 32
BAND = QUAD + 2 * WINDOW
PARTS = 6 * HD
ROWS = PARTS + 3
GROUP = 4
NG = H // GROUP
SLOTS_OF = (((0, 1, 2), (3, 5), (4,)), ((2, 3, 4), (1, 5), (0,)))
NEG = -1e30

REGION = NTOK + P
NTILES = NTOK * TOPK // P + E - 1
SPARE = E - 1
ROW = D + 2
SLOTS = TOPK * NTOK

C_ID, C_MS, C_MT = 0, P, P + 3 * BAND
C_UP = C_MT + 2 * P
C_ONE = C_UP + P
NCB = C_ONE + P
C_IOTA, C_REG = NCB, NCB + E
C_TILE = C_REG + E
C_DEST = C_TILE + NTILES
C_P = C_DEST + NT
NCF = C_P + 1

SHEADS = [(0, 3), (3, 3), (6, 3), (9, 3), (12, 2), (14, 2)]
NS = len(SHEADS)
P_BUFS = 3


def constants():
    c = np.zeros((P, NCF), np.float32)
    p = np.arange(P)
    c[:, C_ID:C_ID + P] = np.eye(P)
    for kind in range(3):
        ms = c[:, C_MS + kind * BAND:C_MS + (kind + 1) * BAND]
        col = np.arange(BAND)[None, :]
        q = (p % QUAD)[:, None]
        ms[(col < q) | (col > q + 2 * WINDOW)] = NEG
        key = (p // QUAD * QUAD)[:, None] - WINDOW + col
        if kind == 0:
            ms[key < 0] = NEG
        if kind == 2:
            ms[key >= P] = NEG
    col = np.arange(2 * P)[None, :]
    mt = c[:, C_MT:C_MT + 2 * P]
    mt[(col < p[:, None]) | (col > p[:, None] + 2 * WINDOW)] = NEG
    c[:, C_UP:C_UP + P] = p[:, None] < p[None, :]
    c[:, C_ONE:C_ONE + P] = 1.0
    c[:, C_IOTA:C_IOTA + E] = np.arange(E)
    c[:, C_REG:C_REG + E] = np.arange(E) * REGION
    c[:, C_TILE:C_TILE + NTILES] = np.arange(NTILES)
    c[:, C_DEST:C_DEST + NT] = TOPK * (np.arange(NT)[None, :] * P + p[:, None])
    c[:, C_P] = p
    pad = np.zeros((E + SPARE, P, ROW), np.float32)
    pad[:, :, D] = SLOTS + np.arange(E + SPARE)[:, None] * P + p[None, :]
    return c, pad


def schedule():
    steps = [("ln1", 0), ("split", 0, 0), ("stack", 0, 0), ("xn", 0), ("vcopy", 0), ("qturn", 0), ("split", 0, 1),
             ("stack", 0, 1), ("ln1", 1), ("xn", 1)]
    between = {6: [("split", 1, 0), ("stack", 1, 0), ("vcopy", 1)], 10: [("qturn", 1)],
               12: [("split", 1, 1), ("stack", 1, 1)]}
    for u in range(NS * TPB):
        steps += [("smax", 0, u)] + between.get(u, [])
    steps += [("mrow", 0), ("mturn", 0)]
    for b in range(B):
        first, last = (1, 12) if b == 0 else (5, 14)
        taken = 0
        for v in range(4 * NG):
            due = taken
            if b + 1 < B and first <= v:
                due = min(NS * TPB, -(-NS * TPB * (v + 1 - first) // (last - first)))
            banks = [("smax", b + 1, u) for u in range(taken, due)]
            taken = due
            steps.append(("score", b, v, 0))
            steps += banks[0:1]
            steps.append(("score", b, v, 1))
            steps += banks[1:2]
            if v >= 1:
                steps.append(("pv", b, v - 1))
                if v % 4 == 0:
                    steps.append(("yout", b, v // 4 - 1))
                if v % 4 == 1 and v > 1:
                    steps.append(("yturn", b, v // 4 - 1))
                    steps.append(("ynorm", b, v // 4 - 1))
            elif b > 0:
                steps.append(("pv", b - 1, 4 * NG - 1))
                steps.append(("yout", b - 1, NG - 1))
            steps += banks[2:]
            if b > 0:
                steps += post(b - 1, v)
            if 2 <= b + 1 < B and v == 0:
                steps += [("stack", b + 1, 0), ("stack", b + 1, 1), ("vcopy", b + 1)]
            if b + 1 < B and v == last - 1:
                steps.append(("mrow", b + 1))
            if b + 1 < B and v == last:
                steps.append(("mturn", b + 1))
            if b + 2 < B:
                steps += {2: [("ln1", b + 2)], 3: [("xn", b + 2)], 4: [("qturn", b + 2)],
                          13: [("split", b + 2, 0)], 14: [("split", b + 2, 1)]}.get(v, [])
    steps.append(("pv", B - 1, 4 * NG - 1))
    steps.append(("yout", B - 1, NG - 1))
    for v in range(4 * NG):
        steps += post(B - 1, v)
    return steps


def post(b, v):
    return {
        1: [("yturn", b, NG - 1), ("ynorm", b, NG - 1)],
        2: [("pturn", b, 0)], 3: [("proj", b, 0)], 4: [("pturn", b, 1)], 5: [("proj", b, 1)],
        6: [("ln2", b)], 7: [("gturn", b, 0)], 8: [("gate", b, 0)], 9: [("gturn", b, 1)], 10: [("gate", b, 1)],
        11: [("top2", b)], 12: [("rank", b)], 13: [("send", b)],
    }.get(v, [])


def build(nc, x, ctx_in, ctx_t, g_xattn, g_ffn, wp, bp, wg, w1, w2, w3, cst, pad, ones, out, xs, yt):
    steps = schedule()
    pm_use = {}
    for step in steps:
        if step[0] in ("mturn", "yturn", "pturn", "proj", "gturn", "gate", "rank"):
            pm_use[step] = len(pm_use) + 1
    with ExitStack() as stack:
        def sb(name, shape, dt=F32):
            return stack.enter_context(nc.sbuf_tensor(name, shape, dt))

        def bank(name, n=1):
            return stack.enter_context(nc.psum_tensor(name, [P, 512 * n], F32))

        def sem(name):
            return stack.enter_context(nc.semaphore(name))

        CF, CB = sb("CF", [P, NCF]), sb("CB", [P, NCB], BF16)
        X = sb("X", [P, NT, D])
        C = sb("C", [P, 2, TPB, D])
        VA = sb("VA", [P, 2, TPB, H, 2 * HD])
        CT = sb("CT", [P, DB, T])
        XN = sb("XN", [P, TPB, DB, HD, H // DB])
        PART = sb("PART", [P, 2, 3, DB, T], BF16)
        RES = sb("RES", [P, DB, T])
        QS = sb("QS", [P, 2, H, T], BF16)
        KS = sb("KS", [P, 2, H, T], BF16)
        PR = sb("PR", [P, P_BUFS, GROUP, 2 * P])
        W1 = sb("W1", [P, E, DB, FI])
        WP, WG, BT = sb("WP", [P, DB, D]), sb("WG", [P, DB, E]), sb("BT", [P, D])
        YS = sb("YS", [P, T])
        YN = sb("YN", [P, TPB, D])
        YR = sb("YR", [P, TPB, GROUP])
        TS = sb("TS", [P, 2, DB, P])
        XR = sb("XR", [P, TPB, TOPK, ROW])
        ST1, MV = sb("ST1", [P, TPB, 6]), sb("MV", [P, B, TPB, 2])
        ST2, MV2 = sb("ST2", [P, TPB, 6]), sb("MV2", [P, TPB, 2])
        VE, RS, HALF = sb("VE", [P, 2, TPB]), sb("RS", [P, B, TPB]), sb("HALF", [P, TPB])
        VE2, RS2 = sb("VE2", [P, TPB]), sb("RS2", [P, TPB])
        GT = sb("GT", [P, 2])
        TG = sb("TG", [P, 2])
        MX, MR = sb("MX", [P, 2, TPB, H]), sb("MR", [P, TPB, H])
        MS = sb("MS", [P, TPB, 3, H], BF16)
        MT = sb("MT", [3 * H, 2, T], BF16)
        SC = sb("SC", [P, TPB, E])
        M8, I8 = sb("M8", [P, TPB, 8]), sb("I8", [P, TPB, 8], U32)
        IDF = sb("IDF", [P, TPB, TOPK])
        OH = sb("OH", [P, TOPK, TPB, E])
        PICK = sb("PICK", [P, TPB, E])
        AB, AC = sb("AB", [P, TPB, E], BF16), sb("AC", [P, TPB + 1, E], BF16)
        DF = sb("DF", [P, TPB])
        EX = sb("EX", [P, TPB])
        G2 = sb("G2", [P, TPB, TOPK])
        SLOT, HIT = sb("SLOT", [P, TPB, E]), sb("HIT", [P, TPB, E])
        POSF, POS = sb("POSF", [P, TPB, TOPK]), sb("POS", [P, TPB, TOPK], U32)
        PPF, PPOS = sb("PPF", [P, E]), sb("PPOS", [P, E], U32)
        CNT, TIL, END = sb("CNT", [P, E]), sb("TIL", [P, E], I32), sb("END", [P, E])
        TILF, ONE8 = sb("TILF", [P, E]), sb("ONE8", [P, E])
        PAST, BEF = sb("PAST", [1, NTILES, E]), sb("BEF", [1, NTILES, E])
        TE, TB, TR = sb("TE", [1, NTILES]), sb("TB", [1, NTILES]), sb("TR", [1, NTILES])
        TX = sb("TX", [1, 2, NTILES], I32)
        DI = sb("DI", [P, 4], U32)

        W2 = KS[:, :, :, :].rearrange("p a h t -> p (a h t)").bitcast(F32).rearrange(
            "p (e b i) -> p e b i", e=E, b=DB)
        W3 = QS[:, :, :, :].rearrange("p a h t -> p (a h t)").bitcast(F32).rearrange(
            "p (e b i) -> p e b i", e=E, b=FB)
        arena = VA[:, :, :, :, :].rearrange("p a t h c -> p (a t h c)")
        SIL = arena[:, 0:2 * FI].rearrange("p (n i) -> p n i", n=2)
        HH = arena[:, 2 * FI:4 * FI].rearrange("p (n i) -> p n i", n=2)
        HT = arena[:, 4 * FI:6 * FI].rearrange("p (n b t) -> p n b t", n=2, b=FB)
        XT = arena[:, 6 * FI:6 * FI + 2 * D].rearrange("p (n b t) -> p n b t", n=2, b=DB)
        arena2 = PR[:, :, :, :].rearrange("p a h t -> p (a h t)")
        XI = arena2[:, 0:4 * ROW].rearrange("p (n r) -> p n r", n=4)
        YO = arena2[:, 4 * ROW:4 * ROW + 4 * D].rearrange("p (n d) -> p n d", n=4)
        PAD = PART[:, :, :, :, :].rearrange("p s n b t -> p (s n b t)").bitcast(F32)[:, 0:E * ROW].rearrange(
            "p (e r) -> p e r", e=E)
        YC = C[:, :, :, :].rearrange("p a t d -> p (a t d)").rearrange("p (n k d) -> p n k d", n=4, k=TOPK)

        PT = [bank("PT0"), bank("PT1")]
        PS = [bank("PS0"), bank("PS1")]
        PK = [bank("PK0"), bank("PK1")]
        PY = bank("PY")
        PM = bank("PM")
        P1, P2 = [PT[0], PS[0]], [PT[1], PS[1]]
        PHT, PXT, PYO = PK, PM, PY

        const_in = sem("const_in")
        x_in = [sem(f"x_in{b}") for b in range(B)]
        ctx_in_ready = [sem(f"ctx_in{b}") for b in range(B)]
        small_in, w1_in, w2_in, w3_in, pad_in, spare_out = (sem(n) for n in (
            "small_in", "w1_in", "w2_in", "w3_in", "pad_in", "spare_out"))
        ones_in, w_in, cb_ready = sem("ones_in"), sem("w_in"), sem("cb_ready")
        setup_done, tanh_done, bias_done = sem("setup_done"), sem("tanh_done"), sem("bias_done")
        pool_step, dve_step, act_step = sem("pool_step"), sem("dve_step"), sem("act_step")
        var_ready, rstd_ready, var2_ready, rstd2_ready = (sem(n) for n in (
            "var_ready", "rstd_ready", "var2_ready", "rstd2_ready"))
        ct_in = [sem(f"ct_in{b}") for b in range(B)]
        xn_ready, q_turned, v_ready, x_biased = sem("xn_ready"), sem("q_turned"), sem("v_ready"), sem("x_biased")
        part1_ready = [sem("k_part1_ready"), sem("q_part1_ready")]
        parts_ready = [sem("k_parts_ready"), sem("q_parts_ready")]
        stack_in = [sem("k_stack_in"), sem("q_stack_in")]
        s_ready, max_taken = sem("s_ready"), sem("max_taken")
        mrow_ready = sem("mrow_ready")
        mrow_in = [sem("mrow_in0"), sem("mrow_in1")]
        k_ready, exp_ready, pv_done = sem("k_ready"), sem("exp_ready"), sem("pv_done")
        y_out = sem("y_out")
        pm_full, pm_free = sem("pm_full"), sem("pm_free")
        xn2_ready, sel_ready, pos_ready, sent = sem("xn2_ready"), sem("sel_ready"), sem("pos_ready"), sem("sent")
        rows_copied = sem("rows_copied")
        diff_ready, ediff_ready = sem("diff_ready"), sem("ediff_ready")
        table_ready, tile_admitted = sem("table_ready"), sem("tile_admitted")
        xi_in = [sem(f"xi_in{i}") for i in range(4)]
        f_xt, f_xts, f_h1, f_sil, f_h2, f_h, f_ht, f_hts, f_y, f_yo, f_dest = (sem(n) for n in (
            "f_xt", "f_xts", "f_h1", "f_sil", "f_h2", "f_h", "f_ht", "f_hts", "f_y", "f_yo", "f_dest"))
        f_sent = [sem(f"f_sent{i}") for i in range(4)]
        yc_in = [sem(f"yc_in{i}") for i in range(4)]
        sum_ready, out_done = sem("sum_ready"), sem("out_done")

        ident = CF[:, C_ID:C_ID + P]
        ident_b = CB[:, C_ID:C_ID + P]
        block = stack.enter_context(nc.Block())

        def keys_of(t, j):
            lo = P * t + QUAD * j - WINDOW
            return max(0, -lo), min(BAND, T - lo), lo

        def queries_of(kt):
            lo, hi = max(0, P * kt - WINDOW), min(T, P * kt + P + WINDOW)
            return lo, hi, lo - (P * kt - WINDOW)

        @block.sync
        def _(sp):
            sp.dma_start(X[:, 0:TPB, :], x[0:T, :].rearrange("(t p) d -> p t d", p=P)).then_inc(x_in[0], 16)
            sp.dma_start(CT[:, :, :], ctx_t[:, :, 0:T]).then_inc(ct_in[0], 16)
            sp.dma_start(CF[:, :], cst[:, :]).then_inc(const_in, 16)
            sp.dma_start(C[:, 0, :, :], ctx_in[0:T, :].rearrange("(t p) d -> p t d", p=P)).then_inc(ctx_in_ready[0], 16)
            sp.dma_start(KS[PARTS:ROWS, :, :, :].rearrange("p a h t -> p (a h t)").bitcast(I32), ones
                         ).then_inc(ones_in, 16)
            sp.dma_start(GT[:, 0:1], g_xattn.partition_broadcast(P)).then_inc(small_in, 16)
            sp.dma_start(GT[:, 1:2], g_ffn.partition_broadcast(P)).then_inc(small_in, 16)
            sp.dma_start(BT[:, :], bp.partition_broadcast(P)).then_inc(small_in, 16)
            for step in steps:
                if step[0] == "split" and step[2] == 0 and step[1] + 1 < B:
                    b = step[1]
                    sp.wait_ge(parts_ready[0], 2 * b + 1)
                    sp.dma_start(CT[:, :, :], ctx_t[:, :, (b + 1) * T:(b + 2) * T]).then_inc(ct_in[b + 1], 16)
                elif step[0] == "stack":
                    b, side = step[1:]
                    if b >= 2:
                        sp.wait_ge(k_ready, 32 * (b - 1))
                    for part, slots in enumerate(SLOTS_OF[side]):
                        if part == 0:
                            sp.wait_ge(part1_ready[side], b + 1)
                        else:
                            sp.wait_ge(parts_ready[side], 2 * b + part)
                        for slot in slots:
                            sp.dma_start((KS, QS)[side][HD * slot:HD * (slot + 1), b % 2, :, :].rearrange(
                                "p h t -> p (h t)"), PART[:, side, part, :, :].rearrange(
                                    "p b t -> p (b t)")).then_inc(stack_in[side], 16)
                    if side == 0 and b == 0:
                        sp.dma_start(X[:, TPB:2 * TPB, :],
                                     x[T:2 * T, :].rearrange("(t p) d -> p t d", p=P)).then_inc(x_in[1], 16)
                    if side == 1 and b == 0:
                        sp.dma_start(C[:, 1, :, :], ctx_in[T:2 * T, :].rearrange(
                            "(t p) d -> p t d", p=P)).then_inc(ctx_in_ready[1], 16)
                        sp.dma_start(WP[:, :, :], wp).then_inc(w_in, 16)
                        sp.dma_start(WG[:, :, :], wg).then_inc(w_in, 16)
                        for later in range(2, B):
                            sp.dma_start(X[:, later * TPB:(later + 1) * TPB, :], x[later * T:(later + 1) * T, :].rearrange(
                                "(t p) d -> p t d", p=P)).then_inc(x_in[later], 16)
                elif step[0] == "mturn":
                    b = step[1]
                    sp.wait_ge(pm_free, pm_use[step])
                    if b >= 2:
                        sp.wait_ge(k_ready, 32 * (b - 1))
                    for part in range(3):
                        sp.dma_start(QS[PARTS + part:PARTS + part + 1, b % 2, :, :],
                                     MT[part * H:(part + 1) * H, b % 2, :]).then_inc(mrow_in[b % 2], 16)
                    if b == 0:
                        sp.dma_start(W1[:, :, :, :], w1).then_inc(w1_in, 16)
                        sp.dma_start(xs[E * REGION:E * REGION + SPARE * P, :],
                                     pad[E:E + SPARE].rearrange("e p r -> (e p) r")).then_inc(spare_out, 16)
                    if b + 2 < B:
                        sp.wait_ge(v_ready, b + 1)
                        sp.dma_start(C[:, b % 2, :, :], ctx_in[(b + 2) * T:(b + 3) * T, :].rearrange(
                            "(t p) d -> p t d", p=P)).then_inc(ctx_in_ready[b + 2], 16)
            for side in range(2):
                sp.wait_ge(stack_in[side], 96 * B)
            sp.dma_start(PAD[:, :, :], pad[0:E].rearrange("e p r -> p e r")).then_inc(pad_in, 16)
            sp.wait_ge(k_ready, 32 * (B - 1))
            half = E // 2
            sp.dma_start(W2[:, 0:half], w2[:, 0:half]).then_inc(w2_in, 16)
            sp.dma_start(W3[:, 0:half], w3[:, 0:half]).then_inc(w3_in, 16)
            sp.wait_ge(k_ready, 32 * B)
            sp.dma_start(W2[:, half:E], w2[:, half:E]).then_inc(w2_in, 16)
            sp.dma_start(W3[:, half:E], w3[:, half:E]).then_inc(w3_in, 16)
            sp.wait_ge(table_ready, 1)
            sp.wait_ge(sent, 16 * (NT * TOPK + E))
            sp.wait_ge(spare_out, 16)

            def load(j, r):
                row = sp.value_load(TX[0:1, 0, bass.ds(j, 1)], min_val=0, max_val=(E * REGION + (SPARE - 1) * P))
                sp.dma_start(XI[:, r, :], xs[bass.ds(row, P), :]).then_inc(xi_in[r], 16)

            def reload(j, r):
                sp.wait_ge(f_dest, j - 3)
                sp.wait_ge(f_yo, j - 3)
                load(j, r)

            for j in range(4):
                load(j, j)
            with sp.Fori(1, NTILES // 4) as i:
                for r in range(4):
                    reload(4 * i + r, r)
            for j in range(NTILES // 4 * 4, NTILES):
                reload(j, j % 4)
            for r in range(4):
                sp.wait_ge(f_sent[r], 16 * ((NTILES - r + 3) // 4))
            for t in range(NT):
                if t >= 4:
                    sp.wait_ge(sum_ready, t - 3)
                sp.dma_start(YC[:, t % 4, :, :], yt[t * P * TOPK:(t + 1) * P * TOPK, :].rearrange(
                    "(p k) d -> p k d", k=TOPK)).then_inc(yc_in[t % 4], 16)
            sp.wait_ge(out_done, 16 * NT)

        @block.gpsimd
        def _(pool):
            done = [0]

            def chain(ins):
                done[0] += 1
                ins.then_inc(pool_step, 1)
                pool.wait_ge(pool_step, done[0])

            pool.memset(HALF[:, :], -0.5).then_inc(setup_done, 1)
            pool.memset(AC[:, 0, :], 0.0).then_inc(setup_done, 1)
            pool.memset(ONE8[:, :], 1.0).then_inc(setup_done, 1)
            pool.wait_ge(setup_done, 3)
            for step in steps:
                kind = step[0]
                if kind == "ln1":
                    b = step[1]
                    pool.wait_ge(var_ready, b + 1)
                    pool.tensor_tensor(RS[:, b, :], VE[:, b % 2, :], HALF[:, :], ALU.pow).then_inc(rstd_ready, 1)
                elif kind == "vcopy":
                    b = step[1]
                    if b == 0:
                        pool.memset(VA[:, :, :, :, HD:2 * HD], 1.0).then_inc(setup_done, 1)
                    pool.wait_ge(ctx_in_ready[b], 16)
                    if b >= 2:
                        pool.wait_ge(pv_done, 16 * (b - 1))
                    pool.tensor_copy(VA[:, b % 2, :, :, 0:HD], C[:, b % 2, :, :].rearrange(
                        "p t (h c) -> p t h c", h=H)).then_inc(v_ready, 1)
                elif kind == "qturn":
                    b = step[1]
                    pool.wait_ge(xn_ready, 4 * (b + 1))
                    pool.wait_ge(bias_done, 1)
                    xt = X[:, 4 * b:4 * b + 4, :]
                    pool.tensor_tensor(xt, xt, BT[:, :].unsqueeze(1).to_broadcast([P, TPB, D]),
                                       ALU.add).then_inc(x_biased, 1)
                elif kind == "ln2":
                    b = step[1]
                    pool.wait_ge(var2_ready, b + 1)
                    pool.tensor_tensor(RS2[:, :], VE2[:, :], HALF[:, :], ALU.pow).then_inc(rstd2_ready, 1)
                    pool.wait_ge(xn2_ready, 4 * (b + 1))
                    pool.tensor_copy(XR[:, :, 1, 0:D], XR[:, :, 0, 0:D]).then_inc(rows_copied, 1)
                elif kind == "send":
                    b = step[1]
                    pool.wait_ge(pos_ready, b + 1)
                    pool.wait_ge(rows_copied, b + 1)
                    for t in range(TPB):
                        for k in range(TOPK):
                            pool.indirect_dma_start(
                                xs[:, :], bass.IndirectOffsetOnAxis(POS[:, t, k:k + 1], 0),
                                XR[:, t, k, :], None).then_inc(sent, 16)
            pool.wait_ge(pad_in, 16)
            pool.wait_ge(table_ready, 1)
            for e in range(E):
                pool.indirect_dma_start(xs[:, :], bass.IndirectOffsetOnAxis(PPOS[:, e:e + 1], 0),
                                        PAD[:, e, :], None).then_inc(sent, 16)

            def scatter(j, r):
                pool.wait_ge(f_dest, j + 1)
                pool.wait_ge(f_yo, j + 1)
                pool.sem_inc(tile_admitted, 1)
                pool.indirect_dma_start(yt[:, :], bass.IndirectOffsetOnAxis(DI[:, r:r + 1], 0),
                                        YO[:, r, :], None).then_inc(f_sent[r], 16)

            with pool.Fori(0, NTILES // 4) as i:
                for r in range(4):
                    scatter(4 * i + r, r)
            for r in range(NTILES % 4):
                scatter(NTILES // 4 * 4 + r, r)

        @block.scalar
        def _(act):
            for step in steps:
                kind = step[0]
                if kind == "split":
                    b, side = step[1:]
                    if b:
                        act.wait_ge(stack_in[side], 96 * b)
                    if side == 0:
                        act.wait_ge(ct_in[b], 16)
                        nc.scalar.activation(PART[:, 0, 0, :, :], CT[:, :, :], ACT.Copy).then_inc(part1_ready[0], 1)
                    else:
                        act.wait_ge(q_turned, 4 * (b + 1))
                        for blk in range(DB):
                            last = nc.scalar.activation(PART[:, 1, 0, blk, :], PT[blk][:, :], ACT.Copy)
                        last.then_inc(part1_ready[1], 1)
                    if (b, side) == (0, 0):
                        act.wait_ge(small_in, 16 * 3)
                        nc.scalar.activation(TG[:, :], GT[:, :], ACT.Tanh).then_inc(tanh_done, 1)
                elif kind == "score":
                    b, v, pair = step[1:]
                    kt, n = v % 4, 16 * b + v
                    lo, hi, _ = queries_of(kt)
                    w = hi - lo
                    if n >= P_BUFS and pair == 0:
                        act.wait_ge(pv_done, n - P_BUFS + 1)
                    act.wait_ge(k_ready, 2 * n + pair + 1)
                    nc.scalar.activation(
                        PR[:, n % P_BUFS, 2 * pair:2 * pair + 2, 0:w],
                        PK[pair][:, 0:2 * w].rearrange("p (h q) -> p h q", h=2),
                        ACT.Exp).then_inc(exp_ready, 1)
                elif kind == "yout":
                    b, g = step[1:]
                    act.wait_ge(pv_done, 16 * b + 4 * g + 4)
                    if b + g > 0:
                        before = 4 * b + g - 1
                        act.wait_ge(pm_free, pm_use["yturn", before // NG, before % NG])
                    nc.scalar.activation(YS[:, :], PY[:, :], ACT.Copy).then_inc(y_out, 1)
                elif kind == "top2":
                    b = step[1]
                    act.wait_ge(diff_ready, b + 1)
                    nc.scalar.activation(EX[:, :], DF[:, :], ACT.Exp).then_inc(ediff_ready, 1)

            def turn_x(j, r):
                act.wait_ge(f_xt, j + 1)
                nc.scalar.activation(XT[:, r % 2, :, :], PXT[:, 0:D].rearrange("p (b t) -> p b t", b=DB),
                                     ACT.Copy).then_inc(f_xts, 1)

            def silu(j, r):
                act.wait_ge(f_h1, j + 1)
                nc.scalar.activation(SIL[:, r % 2, :], P1[r % 2][:, :], ACT.Silu).then_inc(f_sil, 1)

            turn_x(0, 0)
            turn_x(1, 1)
            silu(0, 0)
            with act.Fori(0, (NTILES - 3) // 2) as i:
                for r in range(2):
                    j = 2 * i + r
                    act.wait_ge(f_h, j + 1)
                    silu(j + 1, r + 1)
                    turn_x(j + 2, r)
            j = NTILES - 3
            act.wait_ge(f_h, j + 1)
            silu(j + 1, j + 1)
            turn_x(j + 2, j)
            act.wait_ge(f_h, j + 2)
            silu(j + 2, j + 2)
            for t in range(NT):
                act.wait_ge(sum_ready, t + 1)
                act.dma_start(out[t * P:(t + 1) * P, :], X[:, t, :]).then_inc(out_done, 16)

        @block.vector
        def _(dve):
            done = [0]
            use = [0]

            def chain(ins):
                done[0] += 1
                ins.then_inc(dve_step, 1)
                dve.wait_ge(dve_step, done[0])

            def pm_used():
                use[0] += 1
                dve.wait_ge(pm_full, use[0])

            for step in steps:
                kind = step[0]
                if kind == "ln1":
                    b = step[1]
                    dve.wait_ge(x_in[b], 16)
                    for t in range(TPB):
                        last = nc.vector.bn_stats(ST1[:, t, :], X[:, 4 * b + t, :])
                    chain(last)
                    for t in range(TPB):
                        last = nc.vector.bn_aggr(MV[:, b, t, :], ST1[:, t, :])
                    chain(last)
                    nc.vector.tensor_scalar(VE[:, b % 2, :], MV[:, b, :, 1], EPS, None, ALU.add).then_inc(var_ready, 1)
                    dve.wait_ge(rstd_ready, b + 1)
                    chain(nc.vector.tensor_scalar(RS[:, b, :], RS[:, b, :], Q_SCALE, None, ALU.mult))
                elif kind == "xn":
                    b = step[1]
                    if b:
                        dve.wait_ge(q_turned, 4 * b)
                    for t in range(TPB):
                        nc.vector.tensor_scalar(
                            XN[:, t, :, :, :], X[:, 4 * b + t, :].rearrange("p (h b c) -> p b c h", b=DB, h=H // DB),
                            MV[:, b, t, 0:1], RS[:, b, t:t + 1], ALU.subtract, ALU.mult).then_inc(xn_ready, 1)
                    if b == 0:
                        dve.wait_ge(const_in, 16)
                        nc.vector.tensor_copy(CB[:, :], CF[:, 0:NCB]).then_inc(cb_ready, 1)
                elif kind == "split":
                    b, side = step[1:]
                    dve.wait_ge(part1_ready[side], b + 1)
                    if 2 * b + side:
                        dve.wait_ge(parts_ready[1 - side], 2 * b + 2 * side)
                    one, two, three = (PART[:, side, part, :, :] for part in range(3))
                    if side == 0:
                        chain(nc.vector.tensor_tensor(RES[:, :, :], CT[:, :, :], one, ALU.subtract))
                    else:
                        for blk in range(DB):
                            last = nc.vector.tensor_tensor(RES[:, blk, :], PT[blk][:, :], one[:, blk, :], ALU.subtract)
                        chain(last)
                    nc.vector.tensor_copy(two, RES[:, :, :]).then_inc(parts_ready[side], 1)
                    dve.wait_ge(parts_ready[side], 2 * b + 1)
                    nc.vector.tensor_tensor(three, RES[:, :, :], two, ALU.subtract).then_inc(parts_ready[side], 1)
                    if (b, side) == (0, 1):
                        dve.wait_ge(tanh_done, 1)
                        nc.vector.tensor_scalar(BT[:, :], BT[:, :], TG[:, 0:1], None, ALU.mult).then_inc(bias_done, 1)
                elif kind == "smax":
                    b, t, u = step[1], step[2] // NS, step[2] % NS
                    i = NS * (4 * b + t) + u
                    h0, nh = SHEADS[u]
                    dve.wait_ge(s_ready, i + 1)
                    nc.vector.tensor_reduce(
                        MX[:, b % 2, t, h0:h0 + nh],
                        PS[i % 2][:, 0:nh * BAND].rearrange("p (h c) -> p h c", h=nh),
                        AX.X, ALU.max).then_inc(max_taken, 1)
                elif kind == "mrow":
                    b = step[1]
                    m = MX[:, b % 2, :, :]
                    dve.wait_ge(max_taken, NS * 4 * (b + 1))
                    chain(nc.vector.tensor_scalar(MS[:, :, 0, :], m, -1.0, None, ALU.mult))
                    chain(nc.vector.scalar_tensor_tensor(out=MR[:, :, :], in0=m, scalar=-1.0, in1=MS[:, :, 0, :],
                                                         op0=ALU.mult, op1=ALU.subtract))
                    chain(nc.vector.tensor_copy(MS[:, :, 1, :], MR[:, :, :]))
                    nc.vector.tensor_tensor(MS[:, :, 2, :], MR[:, :, :], MS[:, :, 1, :],
                                            ALU.subtract).then_inc(mrow_ready, 1)
                elif kind == "mturn":
                    b = step[1]
                    pm_used()
                    if b >= 2:
                        dve.wait_ge(mrow_in[b % 2], 48)
                    nc.vector.tensor_copy(MT[:, b % 2, :], PM[0:3 * H, 0:T // 2].bitcast(BF16)
                                          ).then_inc(pm_free, 1)
                elif kind == "ynorm":
                    b, g = step[1:]
                    pm_used()
                    y = PM[:, :].rearrange("p (t h c) -> p t h c", t=TPB, h=GROUP)
                    chain(nc.vector.reciprocal(YR[:, :, :], y[:, :, :, HD]))
                    nc.vector.tensor_tensor(
                        YN[:, :, g * 64:(g + 1) * 64].rearrange("p t (h c) -> p t h c", h=GROUP),
                        y[:, :, :, 0:HD], YR[:, :, :].unsqueeze(3).to_broadcast([P, TPB, GROUP, HD]),
                        ALU.mult).then_inc(pm_free, 1)
                elif kind in ("pturn", "gturn"):
                    pm_used()
                    nc.vector.tensor_copy(TS[:, :, :, :], PM[:, :].rearrange("p (t b q) -> p t b q", t=2, b=DB)
                                          ).then_inc(pm_free, 1)
                elif kind == "proj":
                    b, half = step[1:]
                    i = 4 * b + 2 * half
                    pm_used()
                    nc.vector.scalar_tensor_tensor(
                        out=X[:, i:i + 2, :], in0=PM[:, :].rearrange("p (t d) -> p t d", t=2), scalar=TG[:, 0:1],
                        in1=X[:, i:i + 2, :], op0=ALU.mult, op1=ALU.add).then_inc(pm_free, 1)
                    dve.wait_ge(pm_free, use[0])
                elif kind == "ln2":
                    b = step[1]
                    for t in range(TPB):
                        last = nc.vector.bn_stats(ST2[:, t, :], X[:, 4 * b + t, :])
                    chain(last)
                    for t in range(TPB):
                        last = nc.vector.bn_aggr(MV2[:, t, :], ST2[:, t, :])
                    chain(last)
                    nc.vector.tensor_scalar(VE2[:, :], MV2[:, :, 1], EPS, None, ALU.add).then_inc(var2_ready, 1)
                    dve.wait_ge(rstd2_ready, b + 1)
                    if b >= 1:
                        dve.wait_ge(sent, 16 * TOPK * TPB * b)
                    for t in range(TPB):
                        nc.vector.tensor_scalar(XR[:, t, 0, 0:D], X[:, 4 * b + t, :], MV2[:, t, 0:1],
                                                RS2[:, t:t + 1], ALU.subtract, ALU.mult).then_inc(xn2_ready, 1)
                elif kind == "gate":
                    b, half = step[1:]
                    pm_used()
                    nc.vector.tensor_copy(SC[:, 2 * half:2 * half + 2, :],
                                          PM[:, 0:2 * E].rearrange("p (t e) -> p t e", t=2)).then_inc(pm_free, 1)
                    dve.wait_ge(pm_free, use[0])
                elif kind == "top2":
                    b = step[1]
                    for t in range(TPB):
                        last = nc.vector.max(M8[:, t, :], SC[:, t, :])
                    chain(last)
                    for t in range(TPB):
                        last = nc.vector.max_index(I8[:, t, :], M8[:, t, :], SC[:, t, :])
                    chain(last)
                    nc.vector.tensor_tensor(DF[:, :], M8[:, :, 1], M8[:, :, 0], ALU.subtract).then_inc(diff_ready, 1)
                    chain(nc.vector.tensor_copy(IDF[:, :, :], I8[:, :, 0:TOPK]))
                    iota = CF[:, C_IOTA:C_IOTA + E].unsqueeze(1).to_broadcast([P, TPB, E])
                    for k in range(TOPK):
                        last = nc.vector.tensor_tensor(
                            OH[:, k, :, :], iota, IDF[:, :, k].unsqueeze(2).to_broadcast([P, TPB, E]), ALU.is_equal)
                    chain(last)
                    chain(nc.vector.tensor_tensor(AB[:, :, :], OH[:, 0, :, :], OH[:, 1, :, :], ALU.add))
                    if b >= 1:
                        chain(nc.vector.tensor_copy(AC[:, 0, :], AC[:, TPB, :]))
                    else:
                        dve.wait_ge(setup_done, 3)
                    for t in range(TPB):
                        last = nc.vector.tensor_tensor(AC[:, t + 1, :], AC[:, t, :], AB[:, t, :], ALU.add)
                        if t < TPB - 1:
                            chain(last)
                    last.then_inc(sel_ready, 1)
                    dve.wait_ge(ediff_ready, b + 1)
                    chain(nc.vector.tensor_scalar(DF[:, :], EX[:, :], 1.0, None, ALU.add))
                    chain(nc.vector.reciprocal(G2[:, :, 0], DF[:, :]))
                    chain(nc.vector.tensor_tensor(G2[:, :, 1], G2[:, :, 0], EX[:, :], ALU.mult))
                    chain(nc.vector.tensor_scalar(XR[:, :, :, D + 1], G2[:, :, :], TG[:, 1:2], None, ALU.mult))
                    for k in range(TOPK):
                        last = nc.vector.tensor_scalar(XR[:, :, k, D], CF[:, C_DEST + 4 * b:C_DEST + 4 * b + 4],
                                                       float(k), None, ALU.add)
                    chain(last)
                elif kind == "rank":
                    b = step[1]
                    pm_used()
                    reg = CF[:, C_REG:C_REG + E].unsqueeze(1).to_broadcast([P, TPB, E])
                    if b == B - 1:
                        chain(nc.vector.tensor_copy(CNT[:, :], PM[:, TPB * E:TPB * E + E]))
                    nc.vector.tensor_tensor(SLOT[:, :, :], PM[:, 0:TPB * E].rearrange("p (t e) -> p t e", t=TPB),
                                            reg, ALU.add).then_inc(pm_free, 1)
                    dve.wait_ge(pm_free, use[0])
                    for k in range(TOPK):
                        chain(nc.vector.tensor_tensor(HIT[:, :, :], OH[:, k, :, :], SLOT[:, :, :], ALU.mult))
                        chain(nc.vector.tensor_reduce(POSF[:, :, k], HIT[:, :, :], AX.X, ALU.add))
                    if b >= 1:
                        dve.wait_ge(sent, 16 * TOPK * TPB * b)
                    nc.vector.tensor_copy(POS[:, :, :], POSF[:, :, :]).then_inc(pos_ready, 1)
            chain(nc.vector.tensor_tensor(PPF[:, :], CNT[:, :], CF[:, C_REG:C_REG + E], ALU.add))
            chain(nc.vector.tensor_scalar(PPOS[:, :], PPF[:, :], CF[:, C_P:C_P + 1], None, ALU.add))
            chain(nc.vector.tensor_scalar(TIL[:, :], CNT[:, :], 1.0 / P, (P - 1) / P - (P - 1) / (2 * P),
                                          ALU.mult, ALU.add))
            chain(nc.vector.tensor_copy(TILF[:, :], TIL[:, :]))
            chain(nc.vector.tensor_tensor_scan(END[:, :], ONE8[:, :], TILF[:, :], 0.0, ALU.mult, ALU.add))
            chain(nc.vector.tensor_tensor(
                PAST[:, :, :], CF[0:1, C_TILE:C_TILE + NTILES].unsqueeze(2).to_broadcast([1, NTILES, E]),
                END[0:1, :].unsqueeze(1).to_broadcast([1, NTILES, E]), ALU.is_ge))
            chain(nc.vector.tensor_reduce(TE[:, :], PAST[:, :, :], AX.X, ALU.add))
            chain(nc.vector.tensor_tensor(BEF[:, :, :], PAST[:, :, :],
                                          TILF[0:1, :].unsqueeze(1).to_broadcast([1, NTILES, E]), ALU.mult))
            chain(nc.vector.tensor_reduce(TB[:, :], BEF[:, :, :], AX.X, ALU.add))
            chain(nc.vector.tensor_tensor(TB[:, :], CF[0:1, C_TILE:C_TILE + NTILES], TB[:, :], ALU.subtract))
            chain(nc.vector.tensor_scalar(TB[:, :], TB[:, :], float(P), None, ALU.mult))
            chain(nc.vector.scalar_tensor_tensor(out=TR[:, :], in0=TE[:, :], scalar=float(REGION), in1=TB[:, :],
                                                 op0=ALU.mult, op1=ALU.add))
            chain(nc.vector.tensor_copy(TX[:, 0, :], TR[:, :]))
            nc.vector.tensor_scalar(TX[:, 1, :], TE[:, :], float(E - 1), None, ALU.min).then_inc(table_ready, 1)

            def product(j, r):
                dve.wait_ge(f_sil, j + 1)
                dve.wait_ge(f_h2, j + 1)
                nc.vector.tensor_tensor(HH[:, r % 2, :], SIL[:, r % 2, :], P2[r % 2][:, :], ALU.mult).then_inc(f_h, 1)

            def turn_h(j, r):
                dve.wait_ge(f_ht, j + 1)
                nc.vector.tensor_copy(HT[:, r % 2, :, :],
                                      PHT[r % 2][:, :].rearrange("p (b t) -> p b t", b=FB)).then_inc(f_hts, 1)

            def gated(j, r):
                dve.wait_ge(xi_in[r], xin(j, r))
                nc.vector.tensor_copy(DI[:, r:r + 1], XI[:, r, D:D + 1]).then_inc(f_dest, 1)
                dve.wait_ge(f_y, j + 1)
                nc.vector.tensor_scalar(YO[:, r, :], PYO[:, 0:D], XI[:, r, D + 1:D + 2], None,
                                        ALU.mult).then_inc(f_yo, 1)

            def xin(j, r):
                return 4 * (j - r) + 16

            def step_of(j, r, wait_sent):
                turn_h(j, r)
                product(j + 1, r + 1)
                if wait_sent:
                    dve.wait_ge(f_sent[r % 4], 4 * (j - r % 4))
                gated(j, r % 4)

            product(0, 0)
            for j in range(4):
                step_of(j, j, False)
            with dve.Fori(1, (NTILES - 3) // 4) as i:
                for r in range(4):
                    step_of(4 * i + r, r, True)
            for j in range((NTILES - 3) // 4 * 4, NTILES - 1):
                step_of(j, j % 4, True)
            j = NTILES - 1
            turn_h(j, j)
            dve.wait_ge(f_sent[j % 4], 4 * (j - j % 4))
            gated(j, j % 4)
            for t in range(NT):
                dve.wait_ge(yc_in[t % 4], 16 * (t // 4 + 1))
                chain(nc.vector.tensor_tensor(X[:, t, :], X[:, t, :], YC[:, t % 4, 0, :], ALU.add))
                nc.vector.tensor_tensor(X[:, t, :], X[:, t, :], YC[:, t % 4, 1, :], ALU.add).then_inc(sum_ready, 1)

        @block.tensor
        def _(pe):
            use = [0]

            def pm_take():
                if use[0]:
                    pe.wait_ge(pm_free, use[0])
                use[0] += 1

            pe.wait_ge(const_in, 16)
            for step in steps:
                kind = step[0]
                if kind == "qturn":
                    b = step[1]
                    if b:
                        pe.wait_ge(parts_ready[1], 2 * b - 1)
                    for t in range(TPB):
                        pe.wait_ge(xn_ready, 4 * b + t + 1)
                        for blk in range(DB):
                            last = nc.tensor.transpose(PT[blk][:, t * P:(t + 1) * P],
                                                       XN[:, t, blk, :, :].rearrange("p c h -> p (c h)"), ident)
                        last.then_inc(q_turned, 1)
                elif kind == "smax":
                    b, t, u = step[1], step[2] // NS, step[2] % NS
                    if step == ("smax", 0, 0):
                        pe.wait_ge(cb_ready, 1)
                    if step[2] == 0:
                        pe.wait_ge(stack_in[0], 96 * (b + 1))
                        pe.wait_ge(stack_in[1], 96 * (b + 1))
                    mask = CB[:, C_MS + BAND * (0 if t == 0 else 2 if t == TPB - 1 else 1):][:, 0:BAND]
                    left = 2 * QUAD if t == 0 else QUAD
                    right = BAND - (2 * QUAD if t == TPB - 1 else QUAD)
                    i = NS * (4 * b + t) + u
                    h0, nh = SHEADS[u]
                    if i >= 2:
                        pe.wait_ge(max_taken, i - 1)
                    s = PS[i % 2][:, 0:nh * BAND].rearrange("p (h c) -> p h c", h=nh)
                    for n, (c0, c1) in enumerate(((0, left), (right, BAND))):
                        nc.tensor.matmul(s[:, :, c0:c1], ident_b,
                                         mask[:, c0:c1].unsqueeze(1).to_broadcast([P, nh, c1 - c0]),
                                         start=(n == 0), stop=False, skip_group_check=True)
                    for h in range(nh):
                        for j in range(P // QUAD):
                            c0, c1, lo = keys_of(t, j)
                            q0 = t * P + QUAD * j
                            last = nc.tensor.matmul(s[QUAD * j:QUAD * (j + 1), h, c0:c1],
                                                    QS[0:PARTS, b % 2, h0 + h, q0:q0 + QUAD],
                                                    KS[0:PARTS, b % 2, h0 + h, lo + c0:lo + c1],
                                                    start=False, stop=True, skip_group_check=True)
                    last.then_inc(s_ready, 1)
                elif kind == "mturn":
                    b = step[1]
                    pe.wait_ge(mrow_ready, b + 1)
                    pm_take()
                    for t in range(TPB):
                        last = nc.tensor.transpose(PM[0:3 * H, 64 * t:64 * (t + 1)].bitcast(BF16),
                                                   MS[:, t, :, :].rearrange("p a h -> p (a h)"), ident_b)
                    last.then_inc(pm_full, 1)
                elif kind == "score":
                    b, v, pair = step[1:]
                    g, kt, n = v // 4, v % 4, 16 * b + v
                    lo, hi, c0 = queries_of(kt)
                    w = hi - lo
                    if (v, pair) == (0, 0):
                        pe.wait_ge(mrow_in[b % 2], 48 * (b // 2 + 1))
                        if b == 0:
                            pe.wait_ge(ones_in, 16)
                    if n >= 1:
                        pe.wait_ge(exp_ready, 2 * n + pair - 1)
                    bank_ = PK[pair][:, 0:2 * w].rearrange("p (h q) -> p h q", h=2)
                    nc.tensor.matmul(bank_, ident_b,
                                     CB[:, C_MT + c0:C_MT + c0 + w].unsqueeze(1).to_broadcast([P, 2, w]),
                                     start=True, stop=False, skip_group_check=True)
                    for h in range(2):
                        hh = GROUP * g + 2 * pair + h
                        last = nc.tensor.matmul(bank_[:, h, :], KS[0:ROWS, b % 2, hh, kt * P:(kt + 1) * P],
                                                QS[0:ROWS, b % 2, hh, lo:hi], start=False, stop=(h == 1),
                                                skip_group_check=True)
                    last.then_inc(k_ready, 1)
                elif kind == "pv":
                    b, v = step[1:]
                    g, kt, n = v // 4, v % 4, 16 * b + v
                    lo, hi, _ = queries_of(kt)
                    pe.wait_ge(exp_ready, 2 * n + 2)
                    if v == 0:
                        pe.wait_ge(v_ready, b + 1)
                        if b == 0:
                            pe.wait_ge(setup_done, 4)
                    if kt == 0 and n > 0:
                        pe.wait_ge(y_out, 4 * b + g)
                    for h in range(GROUP):
                        last = nc.tensor.matmul(PY[QUAD * h:QUAD * (h + 1), lo:hi],
                                                VA[:, b % 2, kt, GROUP * g + h, :],
                                                PR[:, n % P_BUFS, h, 0:hi - lo], start=(kt == 0),
                                                stop=(kt == TPB - 1), skip_group_check=True)
                    last.then_inc(pv_done, 1)
                elif kind == "yturn":
                    b, g = step[1:]
                    pe.wait_ge(y_out, 4 * b + g + 1)
                    pm_take()
                    for t in range(TPB):
                        last = nc.tensor.transpose(PM[:, P * t:P * (t + 1)], YS[:, P * t:P * (t + 1)], ident)
                    last.then_inc(pm_full, 1)
                elif kind in ("pturn", "gturn"):
                    b, half = step[1:]
                    if kind == "pturn":
                        pe.wait_ge(pm_free, pm_use["yturn", b, NG - 1])
                    else:
                        pe.wait_ge(xn2_ready, 4 * (b + 1))
                    pm_take()
                    for t in range(2):
                        src = YN[:, 2 * half + t, :] if kind == "pturn" else XR[:, 2 * half + t, 0, 0:D]
                        for blk in range(DB):
                            c = (t * DB + blk) * P
                            last = nc.tensor.transpose(PM[:, c:c + P], src[:, blk * P:(blk + 1) * P], ident)
                    last.then_inc(pm_full, 1)
                elif kind in ("proj", "gate"):
                    if step in (("proj", 0, 0), ("gate", 0, 0)):
                        pe.wait_ge(w_in, 32)
                    pm_take()
                    w, n = (WP, D) if kind == "proj" else (WG, E)
                    for t in range(2):
                        for blk in range(DB):
                            last = nc.tensor.matmul(PM[:, t * n:(t + 1) * n], TS[:, t, blk, :], w[:, blk, :],
                                                    start=(blk == 0), stop=(blk == DB - 1))
                    last.then_inc(pm_full, 1)
                elif kind == "rank":
                    b = step[1]
                    pe.wait_ge(sel_ready, b + 1)
                    pm_take()
                    n = TPB * E
                    nc.tensor.matmul(PM[:, 0:n], CB[:, C_UP:C_UP + P], AB[:, :, :].rearrange("p t e -> p (t e)"),
                                     start=True, stop=False, skip_group_check=True)
                    nc.tensor.matmul(PM[:, 0:n], CB[:, C_ONE:C_ONE + P],
                                     AC[:, 0:TPB, :].rearrange("p t e -> p (t e)"),
                                     start=False, stop=False, skip_group_check=True)
                    nc.tensor.matmul(PM[:, n:n + E], CB[:, C_ONE:C_ONE + P], AC[:, TPB, :],
                                     start=False, stop=True, skip_group_check=True).then_inc(pm_full, 1)

            def turn_x(j, r):
                pe.wait_ge(xi_in[r % 4], 4 * (j - r % 4) + 16)
                for blk in range(DB):
                    last = nc.tensor.transpose(PXT[:, blk * P:(blk + 1) * P], XI[:, r % 4, blk * P:(blk + 1) * P], ident)
                last.then_inc(f_xt, 1)

            def expert(j):
                return pe.value_load(TX[0:1, 1, bass.ds(j, 1)], min_val=0, max_val=E - 1)

            def hidden(w, bank_, e, r, done):
                flat = w.rearrange("p e b i -> p (e b i)")
                for blk in range(DB):
                    last = nc.tensor.matmul(bank_[:, :], XT[:, r % 2, blk, :],
                                            flat[:, bass.ds(e * (DB * FI) + blk * FI, FI)],
                                            start=(blk == 0), stop=(blk == DB - 1))
                last.then_inc(done, 1)

            def turn_h(j, r):
                pe.wait_ge(f_h, j + 1)
                for blk in range(FB):
                    last = nc.tensor.transpose(PHT[r % 2][:, blk * P:(blk + 1) * P],
                                               HH[:, r % 2, blk * P:(blk + 1) * P], ident)
                last.then_inc(f_ht, 1)

            def outputs(j, r, e):
                pe.wait_ge(f_hts, j + 1)
                pe.wait_ge(f_yo, j)
                flat = W3.rearrange("p e b i -> p (e b i)")
                for blk in range(FB):
                    last = nc.tensor.matmul(PYO[:, 0:D], HT[:, r % 2, blk, :],
                                            flat[:, bass.ds(e * (FB * D) + blk * D, D)],
                                            start=(blk == 0), stop=(blk == FB - 1))
                last.then_inc(f_y, 1)

            pe.wait_ge(pm_free, use[0])
            pe.wait_ge(table_ready, 1)
            turn_x(0, 0)
            pe.wait_ge(f_xts, 1)
            turn_x(1, 1)
            pe.wait_ge(w1_in, 16)
            pe.wait_ge(w2_in, 32)
            pe.wait_ge(w3_in, 32)
            e0 = expert(0)
            hidden(W1[:, :, :, :], P1[0], e0, 0, f_h1)
            hidden(W2, P2[0], e0, 0, f_h2)

            def steady(j, r, turn=True):
                e_next = expert(j + 1)
                pe.wait_ge(f_xts, j + 2)
                hidden(W1[:, :, :, :], P1[(r + 1) % 2], e_next, r + 1, f_h1)
                turn_h(j, r)
                if turn:
                    turn_x(j + 2, r + 2)
                hidden(W2, P2[(r + 1) % 2], e_next, r + 1, f_h2)
                outputs(j, r, expert(j))

            n = (NTILES - 3) // 4
            for j in (0, 1, 2, 3):
                steady(j, j)
            with pe.Fori(1, n) as i:
                for r in range(4):
                    steady(4 * i + r, r)
            for j in range(4 * n, NTILES - 1):
                steady(j, j % 4, turn=j + 2 < NTILES)
            j = NTILES - 1
            turn_h(j, j)
            outputs(j, j, expert(j))


_OUT = (B, T, D)


def kernel(**inputs):
    import concourse.bacc as _bacc
    from concourse.bass_utils import run_bass_kernel_spmd as _run

    a = {k: np.asarray(v) for k, v in inputs.items()}

    def rows(w, blocks):
        w = np.swapaxes(w, -1, -2)
        w = w.reshape(*w.shape[:-2], blocks, P, w.shape[-1])
        return np.ascontiguousarray(np.moveaxis(w, -2, 0))

    cst, pad = constants()
    arrays = {
        "x": np.ascontiguousarray(a["x"].reshape(NTOK, D)),
        "ctx_in": np.ascontiguousarray(a["ctx_1024"].reshape(NTOK, D)),
        "ctx_t": np.ascontiguousarray(a["ctx_1024"].reshape(NTOK, H // DB, DB, HD).transpose(3, 1, 2, 0).reshape(
            P, DB, NTOK)),
        "g_xattn": np.ascontiguousarray(a["g_xattn"]),
        "g_ffn": np.ascontiguousarray(a["g_ffn"]),
        "wp": rows(a["L0_xattn_W_proj"], DB),
        "bp": np.ascontiguousarray(a["L0_xattn_b_proj"]),
        "wg": rows(a["L0_ffn_Wg"], DB),
        "w1": rows(a["L0_ffn_W1"], DB),
        "w2": rows(a["L0_ffn_W2"], DB),
        "w3": rows(a["L0_ffn_W3"], FB),
        "cst": cst,
        "pad": pad,
        "ones": np.full((3, B // 2 * H * T // 2), 0x3F803F80, np.int32),
    }
    nc = _bacc.Bacc("TRN2", target_bir_lowering=False, num_devices=1)
    args = {k: nc.dram_tensor(k, v.shape, mybir.dt.from_np(v.dtype), kind="ExternalInput").ap()
            for k, v in arrays.items()}
    out = nc.dram_tensor("out", (NTOK, D), F32, kind="ExternalOutput").ap()
    xs = nc.dram_tensor("xs", (E * REGION + SPARE * P, ROW), F32, kind="Internal").ap()
    yt = nc.dram_tensor("yt", (SLOTS + (E + SPARE) * P, D), F32, kind="Internal").ap()
    build(nc, out=out, xs=xs, yt=yt, **args)
    r = _run(nc, [arrays], core_ids=[0])
    return r.results[0]["out"].reshape(_OUT)
```

```python
from contextlib import ExitStack

import numpy as np
import concourse.bass as bass
from concourse import mybir

F32 = mybir.dt.float32
BF16 = mybir.dt.bfloat16
F16 = mybir.dt.float16
U32 = mybir.dt.uint32
I32 = mybir.dt.int32
ALU = mybir.AluOpType
ACT = mybir.ActivationFunctionType
AX = mybir.AxisListType

P = 128
B, T, D = 4, 512, 256
H, HD, WINDOW = 16, 16, 64
E, FI, TOPK = 8, 512, 2
NTOK = B * T
TPB = T // P
NT = NTOK // P
DB, FB = D // P, FI // P
EPS = 1e-5
Q_SCALE = 1.0 / HD ** 0.5
QUAD = 32
BAND = QUAD + 2 * WINDOW
PARTS = 6 * HD
ROWS = PARTS + 3
GROUP = 4
NG = H // GROUP
SLOTS_OF = (((0, 1, 2), (3, 5), (4,)), ((2, 3, 4), (1, 5), (0,)))
NEG = -1e30

REGION = NTOK + P
NTILES = NTOK * TOPK // P + E - 1
SPARE = E - 1
ROW = D + 2
CHUNK = DB * FI
NCHUNKS = 3 * E
STAGES = (0, 1, 2, 0, 1, 2, 0, 1, 3, 4, 5, 6, 2, 0, 1, 3)


def stage_of(i):
    n = i - E
    before = [m for m in range(n) if STAGES[m] == STAGES[n]]
    return STAGES[n], len(before) + 1, before[-1] + E if before else (E - 1 if STAGES[n] == 2 else None)


X_SCALE = 2.0 ** 11
SPLIT_ORDER = ([(0, e) for e in range(E)] + [(w, e) for w in (1, 2) for e in range(E // 2)] +
               [(w, e) for w in (1, 2) for e in range(E // 2, E)])
SLOTS = TOPK * NTOK

C_ID, C_MS, C_MT = 0, P, P + 3 * BAND
C_UP = C_MT + 2 * P
C_ONE = C_UP + P
NCB = C_ONE + P
C_IOTA, C_REG = NCB, NCB + E
C_TILE = C_REG + E
C_DEST = C_TILE + NTILES
C_P = C_DEST + NT
NCF = C_P + 1

SHEADS = [(0, 3), (3, 3), (6, 3), (9, 3), (12, 2), (14, 2)]
NS = len(SHEADS)
P_BUFS = 3
PAIR = 2


def constants():
    c = np.zeros((P, NCF), np.float32)
    p = np.arange(P)
    c[:, C_ID:C_ID + P] = np.eye(P)
    for kind in range(3):
        ms = c[:, C_MS + kind * BAND:C_MS + (kind + 1) * BAND]
        col = np.arange(BAND)[None, :]
        q = (p % QUAD)[:, None]
        ms[(col < q) | (col > q + 2 * WINDOW)] = NEG
        key = (p // QUAD * QUAD)[:, None] - WINDOW + col
        if kind == 0:
            ms[key < 0] = NEG
        if kind == 2:
            ms[key >= P] = NEG
    col = np.arange(2 * P)[None, :]
    mt = c[:, C_MT:C_MT + 2 * P]
    mt[(col < p[:, None]) | (col > p[:, None] + 2 * WINDOW)] = NEG
    c[:, C_UP:C_UP + P] = p[:, None] < p[None, :]
    c[:, C_ONE:C_ONE + P] = 1.0
    c[:, C_IOTA:C_IOTA + E] = np.arange(E)
    c[:, C_REG:C_REG + E] = np.arange(E) * REGION
    c[:, C_TILE:C_TILE + NTILES] = np.arange(NTILES)
    c[:, C_DEST:C_DEST + NT] = TOPK * (np.arange(NT)[None, :] * P + p[:, None])
    c[:, C_P] = p
    pad = np.zeros((E + SPARE, P, ROW), np.float32)
    pad[:, :, D] = SLOTS + np.arange(E + SPARE)[:, None] * P + p[None, :]
    return c, pad


SCAN_UNIT = ((6, 7, 8, 9, 10, 11, 12, 13), (0, 1, 1, 2, 2, 3, 3, 4), (0, 1, 1, 2, 2, 3, 3, 4))
LOAD_UNIT = ((6, 7, 8, 9, 10, 11, 12, 13), (6, 7, 8, 9, 10, 11, 12, 13))
PREPARE = {2: ["ln1"], 3: ["xn"], 4: ["qturn"], 13: ["kpart1"], 14: ["ksplit", "qpart1"], 15: ["qsplit"]}


def prepare(b, names):
    made = {"kpart1": ("part1", b, 0), "ksplit": ("split", b, 0), "qpart1": ("part1", b, 1), "qsplit": ("split", b, 1)}
    return [made.get(name, (name, b)) for name in names]


def schedule():
    steps = [("ln1", 0), ("part1", 0, 0), ("split", 0, 0), ("stack", 0, 0), ("xn", 0), ("vcopy", 0), ("qturn", 0),
             ("part1", 0, 1), ("split", 0, 1), ("stack", 0, 1), ("ln1", 1), ("xn", 1)]
    between = {2: [("part1", 1, 0)], 6: [("split", 1, 0), ("stack", 1, 0), ("vcopy", 1)],
               10: [("qturn", 1), ("part1", 1, 1)], 13: [("split", 1, 1), ("stack", 1, 1)]}
    for u in range(NS * TPB):
        steps += [("smax", 0, u)] + between.get(u, [])
    steps += [("mrow", 0), ("mturn", 0)]
    splits = 0
    for b in range(B):
        first, last = (1, 10) if b == 0 else (5, 13)
        taken = 0
        for v in range(4 * NG):
            due = taken
            if b + 1 < B and first <= v:
                due = min(NS * TPB, -(-NS * TPB * (v + 1 - first) // (last - first)))
            banks = [("smax", b + 1, u) for u in range(taken, due)]
            taken = due
            steps.append(("score", b, v, 0))
            if b == B - 1 and splits:
                steps.append(("wlow", splits - 1))
            steps += banks[0:1]
            steps.append(("score", b, v, 1))
            steps += banks[1:2]
            if v >= 1:
                steps.append(("pv", b, v - 1))
                if v % 4 == 0:
                    steps.append(("yout", b, v // 4 - 1))
                if v % 4 == 1 and v > 1:
                    steps.append(("yturn", b, v // 4 - 1))
                    steps.append(("ynorm", b, v // 4 - 1))
            elif b > 0:
                steps.append(("pv", b - 1, 4 * NG - 1))
                steps.append(("yout", b - 1, NG - 1))
            steps += banks[2:]
            if b > 0:
                steps += post(b - 1, v)
            if 2 <= b + 1 < B and v == 0:
                steps += [("stack", b + 1, 0), ("stack", b + 1, 1), ("vcopy", b + 1)]
            if b + 1 < B and v == last - 1:
                steps.append(("mrow", b + 1))
            if b + 1 < B and v == last:
                steps.append(("mturn", b + 1))
            if b < B - 1:
                steps += [("wscan", E * b + e) for e in range(E) if SCAN_UNIT[b][e] == v]
                if b < B - 2:
                    steps += [("wload", E * (b + 1) + e) for e in range(E) if LOAD_UNIT[b][e] == v]
                if b == B - 2:
                    steps += {15: [("wpower",)]}.get(v, [])
            else:
                steps += {0: [("wturn",)], 1: [("wcast",)]}.get(v, [])
                if v >= 2:
                    steps.append(("whigh", splits))
                    splits += 1
            if b + 2 < B:
                steps += prepare(b + 2, PREPARE.get(v, []))
    steps.append(("pv", B - 1, 4 * NG - 1))
    steps.append(("yout", B - 1, NG - 1))
    b = B - 1
    highs, lows = iter(range(splits, NCHUNKS)), iter(range(splits - 1, NCHUNKS))
    last = [("yturn", b, NG - 1), "high", ("ynorm", b, NG - 1), ("pturn", b, 0), ("pturn", b, 1), "high", "low", "low",
            ("proj", b, 0), "high", "low", ("proj", b, 1), ("ln2", b), "high", "low", ("xn2", b), "high", "low", ("gturn", b, 0),
            ("gturn", b, 1), "high", ("gate", b, 0), ("gate", b, 1), ("top2", b, 0), ("gates", b, 0), ("rank", b, 0),
            "high", "low", ("scores2", b), ("top2", b, 1), ("gates", b, 1), ("rank", b, 1), ("send", b, 0),
            ("send", b, 1), ("table",)]
    for step in last:
        steps.append(("whigh", next(highs)) if step == "high" else ("wlow", next(lows)) if step == "low" else step)
    steps += [("whigh", i) for i in highs] + [("wlow", i) for i in lows]
    return steps


def routed(b, part):
    if b == B - 1:
        return TPB // 2 * part, TPB // 2 * (part + 1), b + part
    return 0, TPB, b


def post(b, v):
    steps = [[], [("yturn", b, NG - 1), ("ynorm", b, NG - 1)], [("pturn", b, 0)], [("proj", b, 0), ("pturn", b, 1)],
             [("proj", b, 1)], [("ln2", b)], [("xn2", b)], [("gturn", b, 0)], [("gate", b, 0)], [("gturn", b, 1)],
             [("gate", b, 1)], [("top2", b, 0)], [("rank", b, 0), ("gates", b, 0), ("send", b, 0)]]
    return steps[v] if v < len(steps) else []


def build(nc, x, ctx_in, ctx_t, g_xattn, g_ffn, wp, bp, wg, w1, w2, w3, cst, pad, ones, out, xs, yt):
    steps = schedule()
    pm_use = {}
    for step in steps:
        if step[0] in ("wturn", "wcast", "mturn", "yturn", "pturn", "proj", "gturn", "gate", "rank"):
            pm_use[step] = len(pm_use) + 1
    with ExitStack() as stack:
        def sb(name, shape, dt=F32):
            return stack.enter_context(nc.sbuf_tensor(name, shape, dt))

        def bank(name, n=1):
            return stack.enter_context(nc.psum_tensor(name, [P, 512 * n], F32))

        def sem(name):
            return stack.enter_context(nc.semaphore(name))

        CF, CB = sb("CF", [P, NCF]), sb("CB", [P, NCB], BF16)
        X = sb("X", [P, NT, D])
        C = sb("C", [P, 2, TPB, D])
        VA = sb("VA", [P, 2, TPB, H, 2 * HD])
        XN = sb("XN", [P, TPB, DB, HD, H // DB])
        PART = sb("PART", [P, 2, 3, DB, T], BF16)
        RES = sb("RES", [P, DB, T])
        QS = sb("QS", [P, 2, H, T], BF16)
        KS = sb("KS", [P, 2, H, T], BF16)
        PR = sb("PR", [P, P_BUFS, GROUP, 2 * P])
        W1S = sb("W1S", [P, 1 + E, CHUNK])
        CT = W1S[:, 0, :].rearrange("p (b t) -> p b t", b=DB)
        WRAW = W1S[:, 1:1 + E, :]
        WP, WG, BT = sb("WP", [P, DB, D]), sb("WG", [P, DB, E]), sb("BT", [P, D])
        YS = sb("YS", [P, T])
        YN = sb("YN", [P, TPB, D])
        YR = sb("YR", [P, TPB, GROUP])
        TS = sb("TS", [P, 2, DB, P])
        XR = sb("XR", [P, TPB, TOPK, ROW])
        XRH = [XR[:, :, k, 0:D].bitcast(F16) for k in range(TOPK)]
        XN2 = XN[:, :, :, :, :].rearrange("p t b c h -> p t (b c h)")
        ST1, MV = sb("ST1", [P, TPB, 6]), sb("MV", [P, B, TPB, 2])
        ST2, MV2 = sb("ST2", [P, TPB, 6]), sb("MV2", [P, TPB, 2])
        VE, RS, HALF = sb("VE", [P, 2, TPB]), sb("RS", [P, B, TPB]), sb("HALF", [P, TPB])
        VE2, RS2 = sb("VE2", [P, TPB]), sb("RS2", [P, TPB])
        GT = sb("GT", [P, 2])
        TG = sb("TG", [P, 2])
        MX, MR = sb("MX", [P, 2, TPB, H]), sb("MR", [P, TPB, H])
        MS = sb("MS", [P, TPB, 3, H], BF16)
        MT = sb("MT", [3 * H, 2, T], BF16)
        SC = sb("SC", [P, TPB, E])
        M8, I8 = sb("M8", [P, TPB, 8]), sb("I8", [P, TPB, 8], U32)
        IDF = sb("IDF", [P, TPB, TOPK])
        OH = sb("OH", [P, TOPK, TPB, E])
        PICK = sb("PICK", [P, TPB, E])
        AB, AC = sb("AB", [P, TPB, E], BF16), sb("AC", [P, TPB + 1, E], BF16)
        DF = sb("DF", [P, TPB])
        EX = sb("EX", [P, TPB])
        G2 = sb("G2", [P, TPB, TOPK])
        SLOT, HIT = sb("SLOT", [P, TPB, E]), sb("HIT", [P, TPB, E])
        POSF, POS = sb("POSF", [P, TPB, TOPK]), sb("POS", [P, TPB, TOPK], U32)
        MXW, MW = sb("MXW", [P, 3, E]), sb("MW", [P, 3])
        WE = sb("WE", [P, 3], I32)
        EM, DG = sb("EM", [3, 1]), sb("DG", [3, 3])
        WE2 = sb("WE2", [P, 3])
        UP = sb("UP", [P, 3], I32)
        DOWN = sb("DOWN", [P, 3])
        IDH = sb("IDH", [P, P], F16)
        PPOS = sb("PPOS", [1, E], I32)
        CNT, TIL, END = sb("CNT", [P, E]), sb("TIL", [P, E], I32), sb("END", [P, E])
        TILF, ONE8 = sb("TILF", [P, E]), sb("ONE8", [P, E])
        PAST, BEF = sb("PAST", [1, NTILES, E]), sb("BEF", [1, NTILES, E])
        TE, TB, TR = sb("TE", [1, NTILES]), sb("TB", [1, NTILES]), sb("TR", [1, NTILES])
        TX = sb("TX", [1, 2, NTILES], I32)
        DI = sb("DI", [P, 4], U32)

        WF = [W1S[:, :, :].rearrange("p e i -> p (e i)").bitcast(F16),
              KS[:, :, :, :].rearrange("p a h t -> p (a h t)").bitcast(F16),
              QS[:, :, :, :].rearrange("p a h t -> p (a h t)").bitcast(F16)]
        arena = VA[:, :, :, :, :].rearrange("p a t h c -> p (a t h c)")
        STAGE = [C[:, 0, :, :].rearrange("p t d -> p (t d)"), C[:, 1, :, :].rearrange("p t d -> p (t d)"),
                 W1S[:, E, :]] + [arena[:, CHUNK * i:CHUNK * (i + 1)] for i in range(4)]
        SIL = arena[:, 0:2 * FI].rearrange("p (n i) -> p n i", n=2)
        HS = arena[:, 2 * FI:4 * FI].rearrange("p (n i) -> p n i", n=2)
        HH = arena[:, 4 * FI:6 * FI].bitcast(F16).rearrange("p (n s i) -> p n s i", n=2, s=2)
        HT = arena[:, 6 * FI:8 * FI].bitcast(F16).rearrange("p (n s b t) -> p n s b t", n=2, s=2, b=FB)
        arena2 = PR[:, :, :, :].rearrange("p a h t -> p (a h t)")
        XI = arena2[:, 0:4 * ROW].rearrange("p (n r) -> p n r", n=4)
        YO = arena2[:, 4 * ROW:4 * ROW + 4 * D].rearrange("p (n d) -> p n d", n=4)
        XT = arena2[:, 4 * ROW + 4 * D:4 * ROW + 6 * D].bitcast(F16).rearrange("p (n s b t) -> p n s b t", n=2, s=2, b=DB)
        PAD = PART[:, :, :, :, :].rearrange("p s n b t -> p (s n b t)").bitcast(F32)[:, 0:E * ROW].rearrange(
            "p (e r) -> p e r", e=E)
        YC = W1S[:, 0:NT * TOPK * D // CHUNK, :].rearrange("p e i -> p (e i)").rearrange("p (t k d) -> p t k d", t=NT, k=TOPK)

        PT = [bank("PT0"), bank("PT1")]
        PS = [bank("PS0"), bank("PS1")]
        PK = [bank("PK0"), bank("PK1")]
        PY = bank("PY")
        PM = bank("PM")
        tail = {("pturn", B - 1, 0): PT[0], ("pturn", B - 1, 1): PT[1], ("proj", B - 1, 0): PS[0],
                ("proj", B - 1, 1): PS[1], ("gturn", B - 1, 0): PK[0], ("gturn", B - 1, 1): PK[1],
                ("gate", B - 1, 0): PM, ("gate", B - 1, 1): PY,
                ("rank", B - 1, 0): PT[0], ("rank", B - 1, 1): PT[1]}
        for half in range(2):
            tail["pturn", B - 2, half] = tail["gturn", B - 2, half] = PT[half]
            tail["proj", B - 2, half] = tail["gate", B - 2, half] = PS[half]
        tail_ts = [TS, RES[:, :, :].rearrange("p b t -> p (b t)")[:, 0:2 * D].rearrange(
            "p (t b q) -> p t b q", t=2, b=DB)]

        def bank_of(step):
            return tail.get(step, PM)

        def ts_of(step):
            return tail_ts[step[2]] if step in tail else TS

        P1, P2 = [PT[0], PS[0]], [PT[1], PS[1]]
        PHT, PXT, PYO = PK, PM, PY

        const_in = sem("const_in")
        x_in = [sem(f"x_in{b}") for b in range(B)]
        ctx_in_ready = [sem(f"ctx_in{b}") for b in range(B)]
        small_in, pad_in, spare_out = (sem(n) for n in (
            "small_in", "pad_in", "spare_out"))
        ones_in, w_in, cb_ready = sem("ones_in"), sem("w_in"), sem("cb_ready")
        setup_done, tanh_done, bias_done = sem("setup_done"), sem("tanh_done"), sem("bias_done")
        pool_step, dve_step = sem("pool_step"), sem("dve_step")
        var_ready, rstd_ready, var2_ready, rstd2_ready = (sem(n) for n in (
            "var_ready", "rstd_ready", "var2_ready", "rstd2_ready"))
        ct_in = [sem(f"ct_in{b}") for b in range(B)]
        xn_ready, q_turned, v_ready, x_biased = sem("xn_ready"), sem("q_turned"), sem("v_ready"), sem("x_biased")
        part1_ready = [sem("k_part1_ready"), sem("q_part1_ready")]
        parts_ready = [sem("k_parts_ready"), sem("q_parts_ready")]
        stack_in = [sem("k_stack_in"), sem("q_stack_in")]
        s_ready, max_taken = sem("s_ready"), sem("max_taken")
        mrow_ready = sem("mrow_ready")
        mrow_in = [sem("mrow_in0"), sem("mrow_in1")]
        k_ready, exp_ready, pv_done = sem("k_ready"), sem("exp_ready"), sem("pv_done")
        y_out = sem("y_out")
        pm_full, pm_free = sem("pm_full"), sem("pm_free")
        xn2_ready, sel_ready, pos_ready, sent = sem("xn2_ready"), sem("sel_ready"), sem("pos_ready"), sem("sent")
        rows_copied = sem("rows_copied")
        diff_ready, ediff_ready = sem("diff_ready"), sem("ediff_ready")
        ends_ready = sem("ends_ready")
        w_raw_in = [sem(f"w_raw_in{e}") for e in range(E)]
        stage_in = [sem(f"stage_in{i}") for i in range(max(STAGES) + 1)]
        w_scanned, w_power, em_ready, scales_ready, w_high, w_low = (sem(n) for n in (
            "w_scanned", "w_power", "em_ready", "scales_ready", "w_high", "w_low"))
        gates_ready = sem("gates_ready")
        xhigh_ready, xlow_ready = sem("xhigh_ready"), sem("xlow_ready")
        table_ready, tile_admitted = sem("table_ready"), sem("tile_admitted")
        xi_in = [sem(f"xi_in{i}") for i in range(4)]
        f_xt, f_xts, f_h1, f_sil, f_h2, f_hs, f_high, f_low, f_ht, f_hts, f_y, f_yo, f_dest = (sem(n) for n in (
            "f_xt", "f_xts", "f_h1", "f_sil", "f_h2", "f_hs", "f_high", "f_low", "f_ht", "f_hts", "f_y", "f_yo", "f_dest"))
        f_sent = [sem(f"f_sent{i}") for i in range(4)]
        yc_in = [sem(f"yc_in{i}") for i in range(NT // PAIR)]
        sum_ready, out_done = sem("sum_ready"), sem("out_done")

        ident = CF[:, C_ID:C_ID + P]
        ident_b = CB[:, C_ID:C_ID + P]
        block = stack.enter_context(nc.Block())

        def raw(i):
            w, e = SPLIT_ORDER[i]
            return WRAW[:, e, :] if w == 0 else STAGE[stage_of(i)[0]]

        def keys_of(t, j):
            lo = P * t + QUAD * j - WINDOW
            return max(0, -lo), min(BAND, T - lo), lo

        def queries_of(kt):
            lo, hi = max(0, P * kt - WINDOW), min(T, P * kt + P + WINDOW)
            return lo, hi, lo - (P * kt - WINDOW)

        def pad_rows(queue, experts):
            queue.wait_ge(pad_in, 16)
            queue.wait_ge(ends_ready, 1)
            for e in experts:
                row = queue.value_load(PPOS[0:1, e:e + 1], min_val=e * REGION, max_val=e * REGION + NTOK)
                queue.dma_start(xs[bass.ds(row, P), :], PAD[:, e, :]).then_inc(spare_out, 16)

        @block.sync
        def _(sp):
            sp.dma_start(X[:, 0:TPB, :], x[0:T, :].rearrange("(t p) d -> p t d", p=P)).then_inc(x_in[0], 16)
            sp.dma_start(CT[:, :, :], ctx_t[:, :, 0:T]).then_inc(ct_in[0], 16)
            sp.dma_start(CF[:, :], cst[:, :]).then_inc(const_in, 16)
            sp.dma_start(C[:, 0, :, :], ctx_in[0:T, :].rearrange("(t p) d -> p t d", p=P)).then_inc(ctx_in_ready[0], 16)
            sp.dma_start(KS[PARTS:ROWS, :, :, :].rearrange("p a h t -> p (a h t)").bitcast(I32), ones
                         ).then_inc(ones_in, 16)
            sp.dma_start(GT[:, 0:1], g_xattn.partition_broadcast(P)).then_inc(small_in, 16)
            sp.dma_start(GT[:, 1:2], g_ffn.partition_broadcast(P)).then_inc(small_in, 16)
            sp.dma_start(BT[:, :], bp.partition_broadcast(P)).then_inc(small_in, 16)
            for step in steps:
                if step[0] == "wload":
                    i = step[1]
                    sp.wait_ge(w_scanned, i - E + 1)
                    sp.dma_start(WRAW[:, i % E], (w2, w3, w1)[i // E][:, i % E].rearrange(
                        "p b i -> p (b i)")).then_inc(w_raw_in[i % E], 16)
                elif step[0] == "wturn":
                    for side in range(2):
                        sp.wait_ge(stack_in[side], 96 * B)
                    sp.dma_start(PAD[:, :, :], pad[0:E].rearrange("e p r -> p e r")).then_inc(pad_in, 16)
                elif step[0] == "whigh":
                    i = step[1]
                    w, e = SPLIT_ORDER[i]
                    if w == 0:
                        continue
                    if i == E:
                        sp.wait_ge(v_ready, B)
                    stage, _, before = stage_of(i)
                    if before is not None:
                        sp.wait_ge(w_low, before + 1)
                    elif stage >= 3:
                        sp.wait_ge(pv_done, 16 * B)
                    sp.dma_start(STAGE[stage], (w1, w2, w3)[w][:, e].rearrange(
                        "p b i -> p (b i)")).then_inc(stage_in[stage], 16)
                if step[0] == "split" and step[2] == 0 and step[1] + 1 < B:
                    b = step[1]
                    sp.wait_ge(parts_ready[0], 2 * b + 1)
                    sp.dma_start(CT[:, :, :], ctx_t[:, :, (b + 1) * T:(b + 2) * T]).then_inc(ct_in[b + 1], 16)
                elif step[0] == "stack":
                    b, side = step[1:]
                    if b >= 2:
                        sp.wait_ge(k_ready, 32 * (b - 1))
                    for part, slots in enumerate(SLOTS_OF[side]):
                        if part == 0:
                            sp.wait_ge(part1_ready[side], b + 1)
                        else:
                            sp.wait_ge(parts_ready[side], 2 * b + part)
                        for slot in slots:
                            sp.dma_start((KS, QS)[side][HD * slot:HD * (slot + 1), b % 2, :, :].rearrange(
                                "p h t -> p (h t)"), PART[:, side, part, :, :].rearrange(
                                    "p b t -> p (b t)")).then_inc(stack_in[side], 16)
                    if side == 0 and b == 0:
                        sp.dma_start(X[:, TPB:2 * TPB, :],
                                     x[T:2 * T, :].rearrange("(t p) d -> p t d", p=P)).then_inc(x_in[1], 16)
                    if side == 1 and b == 0:
                        sp.dma_start(C[:, 1, :, :], ctx_in[T:2 * T, :].rearrange(
                            "(t p) d -> p t d", p=P)).then_inc(ctx_in_ready[1], 16)
                        sp.dma_start(WP[:, :, :], wp).then_inc(w_in, 16)
                        sp.dma_start(WG[:, :, :], wg).then_inc(w_in, 16)
                        for later in range(2, B):
                            sp.dma_start(X[:, later * TPB:(later + 1) * TPB, :], x[later * T:(later + 1) * T, :].rearrange(
                                "(t p) d -> p t d", p=P)).then_inc(x_in[later], 16)
                elif step[0] == "mturn":
                    b = step[1]
                    sp.wait_ge(pm_free, pm_use[step])
                    if b >= 2:
                        sp.wait_ge(k_ready, 32 * (b - 1))
                    sp.dma_start(QS[PARTS:ROWS, b % 2, :, :], MT[:, b % 2, :]).then_inc(mrow_in[b % 2], 16)
                    if b == 0:
                        for e in range(E):
                            sp.dma_start(WRAW[:, e], w2[:, e].rearrange("p b i -> p (b i)")).then_inc(w_raw_in[e], 16)
                        sp.dma_start(xs[E * REGION:E * REGION + SPARE * P, :],
                                     pad[E:E + SPARE].rearrange("e p r -> (e p) r")).then_inc(spare_out, 16)
                    if b + 2 < B:
                        sp.wait_ge(v_ready, b + 1)
                        sp.dma_start(C[:, b % 2, :, :], ctx_in[(b + 2) * T:(b + 3) * T, :].rearrange(
                            "(t p) d -> p t d", p=P)).then_inc(ctx_in_ready[b + 2], 16)
            pad_rows(sp, range(E // 2))
            sp.wait_ge(table_ready, 1)
            sp.wait_ge(sent, 16 * NT * TOPK)
            sp.wait_ge(spare_out, 16 * (1 + E))

            def load(j, r):
                row = sp.value_load(TX[0:1, 0, bass.ds(j, 1)], min_val=0, max_val=(E * REGION + (SPARE - 1) * P))
                sp.dma_start(XI[:, r, :], xs[bass.ds(row, P), :]).then_inc(xi_in[r], 16)

            def reload(j, r):
                sp.wait_ge(f_dest, j - 3)
                sp.wait_ge(f_yo, j - 3)
                load(j, r)

            for j in range(4):
                load(j, j)
            with sp.Fori(1, NTILES // 4) as i:
                for r in range(4):
                    reload(4 * i + r, r)
            for j in range(NTILES // 4 * 4, NTILES):
                reload(j, j % 4)
            for r in range(4):
                sp.wait_ge(f_sent[r], 16 * ((NTILES - r + 3) // 4))
            sp.wait_ge(f_h1, NTILES)
            for g in range(NT // PAIR):
                sp.dma_start(YC[:, PAIR * g:PAIR * (g + 1), :, :], yt[g * PAIR * P * TOPK:(g + 1) * PAIR * P * TOPK, :].rearrange(
                    "(t p k) d -> p t k d", p=P, k=TOPK)).then_inc(yc_in[g], 16)
            sp.wait_ge(out_done, 16 * (NT // PAIR))

        @block.gpsimd
        def _(pool):
            done = [0]

            def chain(ins):
                done[0] += 1
                ins.then_inc(pool_step, 1)
                pool.wait_ge(pool_step, done[0])

            pool.memset(HALF[:, :], -0.5).then_inc(setup_done, 1)
            pool.memset(AC[:, 0, :], 0.0).then_inc(setup_done, 1)
            pool.memset(ONE8[:, :], 1.0).then_inc(setup_done, 1)
            pool.wait_ge(setup_done, 3)
            for step in steps:
                kind = step[0]
                if kind == "ln1":
                    b = step[1]
                    pool.wait_ge(var_ready, b + 1)
                    pool.tensor_tensor(RS[:, b, :], VE[:, b % 2, :], HALF[:, :], ALU.pow).then_inc(rstd_ready, 1)
                elif kind == "vcopy":
                    b = step[1]
                    if b == 0:
                        pool.memset(VA[:, :, :, :, HD:2 * HD], 1.0).then_inc(setup_done, 1)
                    pool.wait_ge(ctx_in_ready[b], 16)
                    if b >= 2:
                        pool.wait_ge(pv_done, 16 * (b - 1))
                    pool.tensor_copy(VA[:, b % 2, :, :, 0:HD], C[:, b % 2, :, :].rearrange(
                        "p t (h c) -> p t h c", h=H)).then_inc(v_ready, 1)
                elif kind == "qturn":
                    b = step[1]
                    pool.wait_ge(xn_ready, 4 * (b + 1))
                    pool.wait_ge(bias_done, 1)
                    xt = X[:, 4 * b:4 * b + 4, :]
                    pool.tensor_tensor(xt, xt, BT[:, :].unsqueeze(1).to_broadcast([P, TPB, D]),
                                       ALU.add).then_inc(x_biased, 1)
                elif kind == "ln2":
                    b = step[1]
                    pool.wait_ge(var2_ready, b + 1)
                    pool.tensor_tensor(RS2[:, :], VE2[:, :], HALF[:, :], ALU.pow).then_inc(rstd2_ready, 1)
                elif kind == "gturn" and step[2] == 1:
                    b = step[1]
                    pool.wait_ge(xlow_ready, b + 1)
                    pool.tensor_copy(XRH[1][:, :, D:2 * D], XRH[0][:, :, D:2 * D]).then_inc(rows_copied, 1)
                elif kind == "send":
                    b = step[1]
                    t0, t1, n = routed(*step[1:])
                    pool.wait_ge(pos_ready, n + 1)
                    pool.wait_ge(gates_ready, n + 1)
                    pool.wait_ge(rows_copied, b + 1)
                    for t in range(t0, t1):
                        for k in range(TOPK):
                            pool.indirect_dma_start(
                                xs[:, :], bass.IndirectOffsetOnAxis(POS[:, t, k:k + 1], 0),
                                XR[:, t, k, :], None).then_inc(sent, 16)

            def scatter(j, r):
                pool.wait_ge(f_dest, j + 1)
                pool.wait_ge(f_yo, j + 1)
                pool.sem_inc(tile_admitted, 1)
                pool.indirect_dma_start(yt[:, :], bass.IndirectOffsetOnAxis(DI[:, r:r + 1], 0),
                                        YO[:, r, :], None).then_inc(f_sent[r], 16)

            with pool.Fori(0, NTILES // 4) as i:
                for r in range(4):
                    scatter(4 * i + r, r)
            for r in range(NTILES % 4):
                scatter(NTILES // 4 * 4 + r, r)

        @block.scalar
        def _(act):
            for step in steps:
                kind = step[0]
                if kind in ("pturn", "gturn") and step[1] < B - 2:
                    act.wait_ge(pm_full, pm_use[step])
                    nc.scalar.activation(TS[:, :, :, :], PM[:, :].rearrange("p (t b q) -> p t b q", t=2, b=DB),
                                         ACT.Copy).then_inc(pm_free, 1)
                if kind == "part1":
                    b, side = step[1:]
                    if b:
                        act.wait_ge(stack_in[side], 96 * b)
                    if side == 0:
                        act.wait_ge(ct_in[b], 16)
                        nc.scalar.activation(PART[:, 0, 0, :, :], CT[:, :, :], ACT.Copy).then_inc(part1_ready[0], 1)
                    else:
                        act.wait_ge(q_turned, 4 * (b + 1))
                        for blk in range(DB):
                            last = nc.scalar.activation(PART[:, 1, 0, blk, :], PT[blk][:, :], ACT.Copy)
                        last.then_inc(part1_ready[1], 1)
                    if (b, side) == (0, 0):
                        act.wait_ge(small_in, 16 * 3)
                        nc.scalar.activation(TG[:, :], GT[:, :], ACT.Tanh).then_inc(tanh_done, 1)
                elif kind == "score":
                    b, v, pair = step[1:]
                    kt, n = v % 4, 16 * b + v
                    lo, hi, _ = queries_of(kt)
                    w = hi - lo
                    if n >= P_BUFS and pair == 0:
                        act.wait_ge(pv_done, n - P_BUFS + 1)
                    act.wait_ge(k_ready, 2 * n + pair + 1)
                    nc.scalar.activation(
                        PR[:, n % P_BUFS, 2 * pair:2 * pair + 2, 0:w],
                        PK[pair][:, 0:2 * w].rearrange("p (h q) -> p h q", h=2),
                        ACT.Exp).then_inc(exp_ready, 1)
                elif kind == "yout":
                    b, g = step[1:]
                    act.wait_ge(pv_done, 16 * b + 4 * g + 4)
                    if b + g > 0:
                        before = 4 * b + g - 1
                        act.wait_ge(pm_free, pm_use["yturn", before // NG, before % NG])
                    nc.scalar.activation(YS[:, :], PY[:, :], ACT.Copy).then_inc(y_out, 1)
                elif kind == "gturn":
                    b, k = step[1:]
                    act.wait_ge(xn2_ready, 4 * (b + 1))
                    nc.scalar.activation(XRH[k][:, :, 0:D], XN2, ACT.Copy, scale=X_SCALE).then_inc(xhigh_ready, 1)
                elif kind == "whigh":
                    i = step[1]
                    w, e = SPLIT_ORDER[i]
                    if i == 0:
                        act.wait_ge(scales_ready, 1)
                    if i == E:
                        act.wait_ge(k_ready, 32 * (B - 1))
                    if i == 2 * E:
                        act.wait_ge(k_ready, 32 * B)
                    if w == 0:
                        if i >= 1:
                            act.wait_ge(w_low, i)
                    else:
                        act.wait_ge(stage_in[stage_of(i)[0]], 16 * stage_of(i)[1])
                    nc.scalar.activation(WF[w][:, 2 * CHUNK * e:2 * CHUNK * e + CHUNK], raw(i), ACT.Copy,
                                         scale=UP[:, w:w + 1].bitcast(F32)).then_inc(w_high, 1)
                elif kind == "top2":
                    t0, t1, n = routed(*step[1:])
                    act.wait_ge(diff_ready, n + 1)
                    nc.scalar.activation(EX[:, t0:t1], DF[:, t0:t1], ACT.Exp).then_inc(ediff_ready, 1)

            pad_rows(act, range(E // 2, E))

            def turn_x(j, r):
                act.wait_ge(f_xt, j + 1)
                nc.scalar.activation(XT[:, r % 2, :, :, :], PXT[:, 0:D].bitcast(F16).rearrange(
                    "p (s b t) -> p s b t", s=2, b=DB), ACT.Copy).then_inc(f_xts, 1)

            def silu(j, r):
                act.wait_ge(f_h1, j + 1)
                nc.scalar.activation(SIL[:, r % 2, :], P1[r % 2][:, :], ACT.Silu, scale=DOWN[:, 0:1]).then_inc(f_sil, 1)

            def high(j, r, again=True):
                act.wait_ge(f_hs, j + 1)
                if again:
                    act.wait_ge(f_ht, j - 1)
                nc.scalar.activation(HH[:, r % 2, 0, :], HS[:, r % 2, :], ACT.Copy).then_inc(f_high, 1)

            turn_x(0, 0)
            turn_x(1, 1)
            silu(0, 0)
            for j in range(2):
                high(j, j, again=False)
                silu(j + 1, j + 1)
                turn_x(j + 2, j)
            with act.Fori(1, (NTILES - 3) // 2) as i:
                for r in range(2):
                    j = 2 * i + r
                    high(j, r)
                    silu(j + 1, r + 1)
                    turn_x(j + 2, r)
            j = NTILES - 3
            high(j, j)
            silu(j + 1, j + 1)
            turn_x(j + 2, j)
            high(j + 1, j + 1)
            silu(j + 2, j + 2)
            high(j + 2, j + 2)
            for g in range(NT // PAIR):
                act.wait_ge(sum_ready, g + 1)
                act.dma_start(out[g * PAIR * P:(g + 1) * PAIR * P, :].rearrange("(t p) d -> p t d", p=P),
                              X[:, PAIR * g:PAIR * (g + 1), :]).then_inc(out_done, 16)

        @block.vector
        def _(dve):
            done = [0]
            use = [0]

            def chain(ins):
                done[0] += 1
                ins.then_inc(dve_step, 1)
                dve.wait_ge(dve_step, done[0])

            def pm_used():
                use[0] += 1
                dve.wait_ge(pm_full, pm_use[("yturn",) + step[1:] if step[0] == "ynorm" else step])

            def table():
                chain(nc.vector.tensor_scalar(TIL[:, :], CNT[:, :], 1.0 / P, (P - 1) / P - (P - 1) / (2 * P),
                                              ALU.mult, ALU.add))
                chain(nc.vector.tensor_copy(TILF[:, :], TIL[:, :]))
                chain(nc.vector.tensor_tensor_scan(END[:, :], ONE8[:, :], TILF[:, :], 0.0, ALU.mult, ALU.add))
                chain(nc.vector.tensor_tensor(
                    PAST[:, :, :], CF[0:1, C_TILE:C_TILE + NTILES].unsqueeze(2).to_broadcast([1, NTILES, E]),
                    END[0:1, :].unsqueeze(1).to_broadcast([1, NTILES, E]), ALU.is_ge))
                chain(nc.vector.tensor_reduce(TE[:, :], PAST[:, :, :], AX.X, ALU.add))
                chain(nc.vector.tensor_tensor(BEF[:, :, :], PAST[:, :, :],
                                              TILF[0:1, :].unsqueeze(1).to_broadcast([1, NTILES, E]), ALU.mult))
                chain(nc.vector.tensor_reduce(TB[:, :], BEF[:, :, :], AX.X, ALU.add))
                chain(nc.vector.tensor_tensor(TB[:, :], CF[0:1, C_TILE:C_TILE + NTILES], TB[:, :], ALU.subtract))
                chain(nc.vector.tensor_scalar(TB[:, :], TB[:, :], float(P), None, ALU.mult))
                chain(nc.vector.scalar_tensor_tensor(out=TR[:, :], in0=TE[:, :], scalar=float(REGION), in1=TB[:, :],
                                                     op0=ALU.mult, op1=ALU.add))
                chain(nc.vector.tensor_copy(TX[:, 0, :], TR[:, :]))
                nc.vector.tensor_scalar(TX[:, 1, :], TE[:, :], float(E - 1), None, ALU.min).then_inc(table_ready, 1)

            for step in steps:
                kind = step[0]
                if kind == "ln1":
                    b = step[1]
                    dve.wait_ge(x_in[b], 16)
                    for t in range(TPB):
                        last = nc.vector.bn_stats(ST1[:, t, :], X[:, 4 * b + t, :])
                    chain(last)
                    for t in range(TPB):
                        last = nc.vector.bn_aggr(MV[:, b, t, :], ST1[:, t, :])
                    chain(last)
                    nc.vector.tensor_scalar(VE[:, b % 2, :], MV[:, b, :, 1], EPS, None, ALU.add).then_inc(var_ready, 1)
                elif kind == "xn":
                    b = step[1]
                    dve.wait_ge(rstd_ready, b + 1)
                    chain(nc.vector.tensor_scalar(RS[:, b, :], RS[:, b, :], Q_SCALE, None, ALU.mult))
                    if b:
                        dve.wait_ge(q_turned, 4 * b)
                    for t in range(TPB):
                        nc.vector.tensor_scalar(
                            XN[:, t, :, :, :], X[:, 4 * b + t, :].rearrange("p (h b c) -> p b c h", b=DB, h=H // DB),
                            MV[:, b, t, 0:1], RS[:, b, t:t + 1], ALU.subtract, ALU.mult).then_inc(xn_ready, 1)
                    if b == 0:
                        dve.wait_ge(const_in, 16)
                        nc.vector.tensor_copy(CB[:, :], CF[:, 0:NCB]).then_inc(cb_ready, 1)
                        nc.vector.tensor_copy(IDH[:, :], ident).then_inc(cb_ready, 1)
                elif kind == "split":
                    b, side = step[1:]
                    dve.wait_ge(part1_ready[side], b + 1)
                    if 2 * b + side:
                        dve.wait_ge(parts_ready[1 - side], 2 * b + 2 * side)
                    one, two, three = (PART[:, side, part, :, :] for part in range(3))
                    if side == 0:
                        chain(nc.vector.tensor_tensor(RES[:, :, :], CT[:, :, :], one, ALU.subtract))
                    else:
                        for blk in range(DB):
                            last = nc.vector.tensor_tensor(RES[:, blk, :], PT[blk][:, :], one[:, blk, :], ALU.subtract)
                        chain(last)
                    nc.vector.tensor_copy(two, RES[:, :, :]).then_inc(parts_ready[side], 1)
                    dve.wait_ge(parts_ready[side], 2 * b + 1)
                    nc.vector.tensor_tensor(three, RES[:, :, :], two, ALU.subtract).then_inc(parts_ready[side], 1)
                    if (b, side) == (0, 1):
                        dve.wait_ge(tanh_done, 1)
                        nc.vector.tensor_scalar(BT[:, :], BT[:, :], TG[:, 0:1], None, ALU.mult).then_inc(bias_done, 1)
                elif kind == "smax":
                    b, t, u = step[1], step[2] // NS, step[2] % NS
                    i = NS * (4 * b + t) + u
                    h0, nh = SHEADS[u]
                    dve.wait_ge(s_ready, i + 1)
                    nc.vector.tensor_reduce(
                        MX[:, b % 2, t, h0:h0 + nh],
                        PS[i % 2][:, 0:nh * BAND].rearrange("p (h c) -> p h c", h=nh),
                        AX.X, ALU.max).then_inc(max_taken, 1)
                elif kind == "mrow":
                    b = step[1]
                    m = MX[:, b % 2, :, :]
                    dve.wait_ge(max_taken, NS * 4 * (b + 1))
                    chain(nc.vector.tensor_scalar(MS[:, :, 0, :], m, -1.0, None, ALU.mult))
                    chain(nc.vector.scalar_tensor_tensor(out=MR[:, :, :], in0=m, scalar=-1.0, in1=MS[:, :, 0, :],
                                                         op0=ALU.mult, op1=ALU.subtract))
                    chain(nc.vector.tensor_copy(MS[:, :, 1, :], MR[:, :, :]))
                    nc.vector.tensor_tensor(MS[:, :, 2, :], MR[:, :, :], MS[:, :, 1, :],
                                            ALU.subtract).then_inc(mrow_ready, 1)
                elif kind == "mturn":
                    b = step[1]
                    pm_used()
                    if b >= 2:
                        dve.wait_ge(mrow_in[b % 2], 16)
                    nc.vector.tensor_copy(MT[:, b % 2, :], PM[0:3 * H, 0:T // 2].bitcast(BF16)
                                          ).then_inc(pm_free, 1)
                elif kind == "ynorm":
                    b, g = step[1:]
                    pm_used()
                    y = PM[:, :].rearrange("p (t h c) -> p t h c", t=TPB, h=GROUP)
                    chain(nc.vector.reciprocal(YR[:, :, :], y[:, :, :, HD]))
                    nc.vector.tensor_tensor(
                        YN[:, :, g * 64:(g + 1) * 64].rearrange("p t (h c) -> p t h c", h=GROUP),
                        y[:, :, :, 0:HD], YR[:, :, :].unsqueeze(3).to_broadcast([P, TPB, GROUP, HD]),
                        ALU.mult).then_inc(pm_free, 1)
                elif kind in ("pturn", "gturn") and step[1] < B - 2:
                    use[0] += 1
                elif kind in ("pturn", "gturn"):
                    pm_used()
                    nc.vector.tensor_copy(ts_of(step)[:, :, :, :], bank_of(step)[:, :].rearrange("p (t b q) -> p t b q", t=2, b=DB)
                                          ).then_inc(pm_free, 1)
                elif kind == "proj":
                    b, half = step[1:]
                    i = 4 * b + 2 * half
                    pm_used()
                    nc.vector.scalar_tensor_tensor(
                        out=X[:, i:i + 2, :], in0=bank_of(step)[:, :].rearrange("p (t d) -> p t d", t=2), scalar=TG[:, 0:1],
                        in1=X[:, i:i + 2, :], op0=ALU.mult, op1=ALU.add).then_inc(pm_free, 1)
                    dve.wait_ge(pm_free, use[0])
                elif kind == "ln2":
                    b = step[1]
                    for t in range(TPB):
                        last = nc.vector.bn_stats(ST2[:, t, :], X[:, 4 * b + t, :])
                    chain(last)
                    for t in range(TPB):
                        last = nc.vector.bn_aggr(MV2[:, t, :], ST2[:, t, :])
                    chain(last)
                    nc.vector.tensor_scalar(VE2[:, :], MV2[:, :, 1], EPS, None, ALU.add).then_inc(var2_ready, 1)
                elif kind == "xn2":
                    b = step[1]
                    dve.wait_ge(rstd2_ready, b + 1)
                    dve.wait_ge(q_turned, 4 * min(b + 3, B))
                    if b >= 1:
                        dve.wait_ge(sent, 16 * TOPK * TPB * b)
                    for t in range(TPB):
                        nc.vector.tensor_scalar(XN2[:, t, :], X[:, 4 * b + t, :], MV2[:, t, 0:1],
                                                RS2[:, t:t + 1], ALU.subtract, ALU.mult).then_inc(xn2_ready, 1)
                elif kind == "wscan":
                    i = step[1]
                    dve.wait_ge(w_raw_in[i % E], 16 * (i // E + 1))
                    nc.vector.tensor_reduce(MXW[:, (i // E + 1) % 3, i % E:i % E + 1], WRAW[:, i % E], AX.X, ALU.max,
                                            apply_absolute_value=True).then_inc(w_scanned, 1)
                elif kind == "wpower":
                    dve.wait_ge(w_scanned, NCHUNKS)
                    chain(nc.vector.tensor_reduce(MW[:, :], MXW[:, :, :], AX.X, ALU.max))
                    chain(nc.vector.tensor_scalar(MW[:, :], MW[:, :], 2.0 ** -30, None, ALU.max))
                    nc.vector.tensor_scalar(WE[:, :], MW[:, :].bitcast(I32), 0x7F800000, None,
                                            ALU.bitwise_and).then_inc(w_power, 1)
                elif kind == "wturn":
                    pm_used()
                    nc.vector.tensor_reduce(EM[:, :], PM[0:3, 0:P], AX.X, ALU.max).then_inc(pm_free, 1)
                    dve.wait_ge(pm_free, use[0])
                    nc.vector.tensor_scalar(DG[:, :], CF[0:3, C_ID:C_ID + 3], EM[:, 0:1], None,
                                            ALU.mult).then_inc(em_ready, 1)
                elif kind == "wcast":
                    pm_used()
                    nc.vector.tensor_copy(WE2[:, :], PM[:, 0:3]).then_inc(pm_free, 1)
                    dve.wait_ge(pm_free, use[0])
                    chain(nc.vector.tensor_scalar(UP[:, :], WE2[:, :].bitcast(I32), -1.0,
                                                  float((2 * 127 + 14) << 23), ALU.mult, ALU.add))
                    nc.vector.tensor_scalar(DOWN[:, 0:1], WE2[:, 0:1], 2.0 ** -14 / X_SCALE, None, ALU.mult)
                    nc.vector.tensor_scalar(DOWN[:, 1:2], UP[:, 0:1].bitcast(F32), 2.0 ** -15 / (D * D * X_SCALE), None,
                                            ALU.mult)
                    chain(nc.vector.tensor_tensor(DOWN[:, 2:3], WE2[:, 1:2], WE2[:, 2:3], ALU.mult))
                    nc.vector.tensor_scalar(DOWN[:, 2:3], DOWN[:, 2:3], WE2[:, 0:1], 2.0 ** -27 * D * D,
                                            ALU.mult, ALU.mult).then_inc(scales_ready, 1)
                elif kind == "wlow":
                    i = step[1]
                    w, e = SPLIT_ORDER[i]
                    at = 2 * CHUNK * e
                    dve.wait_ge(w_high, i + 1)
                    nc.vector.scalar_tensor_tensor(
                        out=WF[w][:, at + CHUNK:at + 2 * CHUNK], in0=raw(i),
                        scalar=UP[:, w:w + 1].bitcast(F32), in1=WF[w][:, at:at + CHUNK],
                        op0=ALU.mult, op1=ALU.subtract).then_inc(w_low, 1)
                elif kind == "table":
                    table()
                elif step == ("gate", B - 1, 1):
                    pass
                elif kind in ("gate", "scores2"):
                    if kind == "scores2":
                        step = ("gate", B - 1, 1)
                    b, half = step[1:]
                    if half == 0:
                        dve.wait_ge(xhigh_ready, 2 * b + 1)
                        nc.vector.scalar_tensor_tensor(
                            out=XRH[0][:, :, D:2 * D], in0=XN2, scalar=X_SCALE, in1=XRH[0][:, :, 0:D],
                            op0=ALU.mult, op1=ALU.subtract).then_inc(xlow_ready, 1)
                    pm_used()
                    nc.vector.tensor_copy(SC[:, 2 * half:2 * half + 2, :],
                                          bank_of(step)[:, 0:2 * E].rearrange("p (t e) -> p t e", t=2)).then_inc(pm_free, 1)
                    dve.wait_ge(pm_free, use[0])
                elif kind == "top2":
                    b = step[1]
                    t0, t1, n = routed(*step[1:])
                    nt = t1 - t0
                    for t in range(t0, t1):
                        last = nc.vector.max(M8[:, t, :], SC[:, t, :])
                    chain(last)
                    for t in range(t0, t1):
                        last = nc.vector.max_index(I8[:, t, :], M8[:, t, :], SC[:, t, :])
                    chain(last)
                    nc.vector.tensor_tensor(DF[:, t0:t1], M8[:, t0:t1, 1], M8[:, t0:t1, 0],
                                            ALU.subtract).then_inc(diff_ready, 1)
                    chain(nc.vector.tensor_copy(IDF[:, t0:t1, :], I8[:, t0:t1, 0:TOPK]))
                    iota = CF[:, C_IOTA:C_IOTA + E].unsqueeze(1).to_broadcast([P, nt, E])
                    for k in range(TOPK):
                        last = nc.vector.tensor_tensor(
                            OH[:, k, t0:t1, :], iota, IDF[:, t0:t1, k].unsqueeze(2).to_broadcast([P, nt, E]),
                            ALU.is_equal)
                    chain(last)
                    chain(nc.vector.tensor_tensor(AB[:, t0:t1, :], OH[:, 0, t0:t1, :], OH[:, 1, t0:t1, :], ALU.add))
                    if t0 > 0:
                        pass
                    elif b >= 1:
                        chain(nc.vector.tensor_copy(AC[:, 0, :], AC[:, TPB, :]))
                    else:
                        dve.wait_ge(setup_done, 3)
                    for t in range(t0, t1):
                        last = nc.vector.tensor_tensor(AC[:, t + 1, :], AC[:, t, :], AB[:, t, :], ALU.add)
                        if t < t1 - 1:
                            chain(last)
                    last.then_inc(sel_ready, 1)
                elif kind == "gates":
                    b = step[1]
                    t0, t1, n = routed(*step[1:])
                    dve.wait_ge(ediff_ready, n + 1)
                    chain(nc.vector.tensor_scalar(DF[:, t0:t1], EX[:, t0:t1], 1.0, None, ALU.add))
                    chain(nc.vector.reciprocal(G2[:, t0:t1, 0], DF[:, t0:t1]))
                    chain(nc.vector.tensor_tensor(G2[:, t0:t1, 1], G2[:, t0:t1, 0], EX[:, t0:t1], ALU.mult))
                    chain(nc.vector.tensor_scalar(XR[:, t0:t1, :, D + 1], G2[:, t0:t1, :], TG[:, 1:2], None, ALU.mult))
                    for k in range(TOPK):
                        last = nc.vector.tensor_scalar(XR[:, t0:t1, k, D], CF[:, C_DEST + 4 * b + t0:C_DEST + 4 * b + t1],
                                                       float(k), None, ALU.add)
                    last.then_inc(gates_ready, 1)
                elif kind == "rank":
                    b = step[1]
                    t0, t1, _ = routed(*step[1:])
                    nt, bank_ = t1 - t0, bank_of(step)
                    pm_used()
                    reg = CF[:, C_REG:C_REG + E].unsqueeze(1).to_broadcast([P, nt, E])
                    if b == B - 1 and t1 == TPB:
                        chain(nc.vector.tensor_copy(CNT[:, :], bank_[:, nt * E:nt * E + E]))
                        nc.vector.tensor_tensor(PPOS[:, :], CNT[0:1, :], CF[0:1, C_REG:C_REG + E],
                                                ALU.add).then_inc(ends_ready, 1)
                    nc.vector.tensor_tensor(SLOT[:, t0:t1, :], bank_[:, 0:nt * E].rearrange("p (t e) -> p t e", t=nt),
                                            reg, ALU.add).then_inc(pm_free, 1)
                    dve.wait_ge(pm_free, use[0])
                    for k in range(TOPK):
                        chain(nc.vector.tensor_tensor(HIT[:, t0:t1, :], OH[:, k, t0:t1, :], SLOT[:, t0:t1, :], ALU.mult))
                        chain(nc.vector.tensor_reduce(POSF[:, t0:t1, k], HIT[:, t0:t1, :], AX.X, ALU.add))
                    if b >= 1:
                        dve.wait_ge(sent, 16 * TOPK * TPB * b)
                    nc.vector.tensor_copy(POS[:, t0:t1, :], POSF[:, t0:t1, :]).then_inc(pos_ready, 1)
            def product(j, r, again=True):
                dve.wait_ge(f_sil, j + 1)
                dve.wait_ge(f_h2, j + 1)
                if again:
                    dve.wait_ge(f_low, j - 1)
                nc.vector.scalar_tensor_tensor(out=HS[:, r % 2, :], in0=P2[r % 2][:, :], scalar=DOWN[:, 1:2],
                                               in1=SIL[:, r % 2, :], op0=ALU.mult, op1=ALU.mult).then_inc(f_hs, 1)
                dve.wait_ge(f_high, j + 1)
                nc.vector.tensor_tensor(HH[:, r % 2, 1, :], HS[:, r % 2, :], HH[:, r % 2, 0, :],
                                        ALU.subtract).then_inc(f_low, 1)

            def turn_h(j, r):
                dve.wait_ge(f_ht, j + 1)
                nc.vector.tensor_copy(HT[:, r % 2, :, :, :], PHT[r % 2][:, :].bitcast(F16).rearrange(
                    "p (s b t) -> p s b t", s=2, b=FB)).then_inc(f_hts, 1)

            def gated(j, r):
                dve.wait_ge(xi_in[r], xin(j, r))
                nc.vector.tensor_copy(DI[:, r:r + 1], XI[:, r, D:D + 1]).then_inc(f_dest, 1)
                dve.wait_ge(f_y, j + 1)
                nc.vector.tensor_scalar(YO[:, r, :], PYO[:, 0:D], XI[:, r, D + 1:D + 2], DOWN[:, 2:3],
                                        ALU.mult, ALU.mult).then_inc(f_yo, 1)

            def xin(j, r):
                return 4 * (j - r) + 16

            def step_of(j, r, wait_sent, again=True):
                turn_h(j, r)
                product(j + 1, r + 1, again)
                if wait_sent:
                    dve.wait_ge(f_sent[r % 4], 4 * (j - r % 4))
                gated(j, r % 4)

            product(0, 0, False)
            for j in range(4):
                step_of(j, j, False, again=(j > 0))
            with dve.Fori(1, (NTILES - 3) // 4) as i:
                for r in range(4):
                    step_of(4 * i + r, r, True)
            for j in range((NTILES - 3) // 4 * 4, NTILES - 1):
                step_of(j, j % 4, True)
            j = NTILES - 1
            turn_h(j, j)
            dve.wait_ge(f_sent[j % 4], 4 * (j - j % 4))
            gated(j, j % 4)
            for g in range(NT // PAIR):
                dve.wait_ge(yc_in[g], 16)
                xt, yk = X[:, PAIR * g:PAIR * (g + 1), :], YC[:, PAIR * g:PAIR * (g + 1), :, :]
                chain(nc.vector.tensor_tensor(xt, xt, yk[:, :, 0, :], ALU.add))
                nc.vector.tensor_tensor(xt, xt, yk[:, :, 1, :], ALU.add).then_inc(sum_ready, 1)

        @block.tensor
        def _(pe):
            use, last_use = [0], [0]

            def pm_take():
                if last_use[0]:
                    pe.wait_ge(pm_free, last_use[0])
                use[0] += 1
                last_use[0] = use[0]

            def keep_warm(n):
                for _ in range(n):
                    nc.tensor.matmul(PY[:, :], ident_b, CB[:, 0:512], start=True, stop=True)

            pe.wait_ge(const_in, 16)
            for step in steps:
                kind = step[0]
                if kind == "qturn":
                    b = step[1]
                    if b:
                        pe.wait_ge(parts_ready[1], 2 * b - 1)
                    for t in range(TPB):
                        pe.wait_ge(xn_ready, 4 * b + t + 1)
                        for blk in range(DB):
                            last = nc.tensor.transpose(PT[blk][:, t * P:(t + 1) * P],
                                                       XN[:, t, blk, :, :].rearrange("p c h -> p (c h)"), ident)
                        last.then_inc(q_turned, 1)
                elif kind == "smax":
                    b, t, u = step[1], step[2] // NS, step[2] % NS
                    if step == ("smax", 0, 0):
                        pe.wait_ge(cb_ready, 1)
                        keep_warm(10)
                        pe.wait_ge(parts_ready[1], 2)
                        keep_warm(22)
                    if step[2] == 0:
                        pe.wait_ge(stack_in[0], 96 * (b + 1))
                        pe.wait_ge(stack_in[1], 96 * (b + 1))
                    mask = CB[:, C_MS + BAND * (0 if t == 0 else 2 if t == TPB - 1 else 1):][:, 0:BAND]
                    left = 2 * QUAD if t == 0 else QUAD
                    right = BAND - (2 * QUAD if t == TPB - 1 else QUAD)
                    i = NS * (4 * b + t) + u
                    h0, nh = SHEADS[u]
                    if i >= 2:
                        pe.wait_ge(max_taken, i - 1)
                    s = PS[i % 2][:, 0:nh * BAND].rearrange("p (h c) -> p h c", h=nh)
                    for n, (c0, c1) in enumerate(((0, left), (right, BAND))):
                        nc.tensor.matmul(s[:, :, c0:c1], ident_b,
                                         mask[:, c0:c1].unsqueeze(1).to_broadcast([P, nh, c1 - c0]),
                                         start=(n == 0), stop=False, skip_group_check=True)
                    for h in range(nh):
                        for j in range(P // QUAD):
                            c0, c1, lo = keys_of(t, j)
                            q0 = t * P + QUAD * j
                            last = nc.tensor.matmul(s[QUAD * j:QUAD * (j + 1), h, c0:c1],
                                                    QS[0:PARTS, b % 2, h0 + h, q0:q0 + QUAD],
                                                    KS[0:PARTS, b % 2, h0 + h, lo + c0:lo + c1],
                                                    start=False, stop=True, skip_group_check=True)
                    last.then_inc(s_ready, 1)
                elif kind == "mturn":
                    b = step[1]
                    pe.wait_ge(mrow_ready, b + 1)
                    pm_take()
                    for t in range(TPB):
                        last = nc.tensor.transpose(PM[0:3 * H, 64 * t:64 * (t + 1)].bitcast(BF16),
                                                   MS[:, t, :, :].rearrange("p a h -> p (a h)"), ident_b)
                    last.then_inc(pm_full, 1)
                elif kind == "split" and step[1] == 1:
                    keep_warm(12)
                elif kind == "wturn":
                    pe.wait_ge(w_power, 1)
                    pm_take()
                    nc.tensor.transpose(PM[0:3, 0:P], WE[:, :].bitcast(F32), ident).then_inc(pm_full, 1)
                elif kind == "wcast":
                    pe.wait_ge(em_ready, 1)
                    pm_take()
                    nc.tensor.matmul(PM[:, 0:3], CF[0:3, C_ONE:C_ONE + P], DG[:, :], start=True,
                                     stop=True).then_inc(pm_full, 1)
                elif kind == "score":
                    b, v, pair = step[1:]
                    g, kt, n = v // 4, v % 4, 16 * b + v
                    lo, hi, c0 = queries_of(kt)
                    w = hi - lo
                    if (v, pair) == (0, 0):
                        pe.wait_ge(mrow_in[b % 2], 16 * (b // 2 + 1))
                        if b == 0:
                            pe.wait_ge(ones_in, 16)
                    if n >= 1:
                        pe.wait_ge(exp_ready, 2 * n + pair - 1)
                    bank_ = PK[pair][:, 0:2 * w].rearrange("p (h q) -> p h q", h=2)
                    nc.tensor.matmul(bank_, ident_b,
                                     CB[:, C_MT + c0:C_MT + c0 + w].unsqueeze(1).to_broadcast([P, 2, w]),
                                     start=True, stop=False, skip_group_check=True)
                    for h in range(2):
                        hh = GROUP * g + 2 * pair + h
                        last = nc.tensor.matmul(bank_[:, h, :], KS[0:ROWS, b % 2, hh, kt * P:(kt + 1) * P],
                                                QS[0:ROWS, b % 2, hh, lo:hi], start=False, stop=(h == 1),
                                                skip_group_check=True)
                    last.then_inc(k_ready, 1)
                elif kind == "pv":
                    b, v = step[1:]
                    g, kt, n = v // 4, v % 4, 16 * b + v
                    lo, hi, _ = queries_of(kt)
                    pe.wait_ge(exp_ready, 2 * n + 2)
                    if v == 0:
                        pe.wait_ge(v_ready, b + 1)
                        if b == 0:
                            pe.wait_ge(setup_done, 4)
                    if kt == 0 and n > 0:
                        pe.wait_ge(y_out, 4 * b + g)
                    for h in range(GROUP):
                        last = nc.tensor.matmul(PY[QUAD * h:QUAD * (h + 1), lo:hi],
                                                VA[:, b % 2, kt, GROUP * g + h, :],
                                                PR[:, n % P_BUFS, h, 0:hi - lo], start=(kt == 0),
                                                stop=(kt == TPB - 1), skip_group_check=True)
                    last.then_inc(pv_done, 1)
                elif kind == "yturn":
                    b, g = step[1:]
                    pe.wait_ge(y_out, 4 * b + g + 1)
                    pm_take()
                    for t in range(TPB):
                        last = nc.tensor.transpose(PM[:, P * t:P * (t + 1)], YS[:, P * t:P * (t + 1)], ident)
                    last.then_inc(pm_full, 1)
                elif kind in ("pturn", "gturn"):
                    b, half = step[1:]
                    if kind == "pturn":
                        pe.wait_ge(pm_free, pm_use["yturn", b, NG - 1])
                    elif b == B - 1:
                        pe.wait_ge(xn2_ready, 4 * b + 2 * half + 2)
                    else:
                        pe.wait_ge(xn2_ready, 4 * (b + 1))
                    if step in tail:
                        use[0] += 1
                    else:
                        pm_take()
                    for t in range(2):
                        src = YN[:, 2 * half + t, :] if kind == "pturn" else XN2[:, 2 * half + t, :]
                        for blk in range(DB):
                            c = (t * DB + blk) * P
                            last = nc.tensor.transpose(bank_of(step)[:, c:c + P], src[:, blk * P:(blk + 1) * P], ident)
                    last.then_inc(pm_full, 1)
                elif kind in ("proj", "gate"):
                    if step in (("proj", 0, 0), ("gate", 0, 0)):
                        pe.wait_ge(w_in, 32)
                    if step in tail:
                        use[0] += 1
                        turn = ("pturn" if kind == "proj" else "gturn", step[1], step[2])
                        pe.wait_ge(pm_free, pm_use[turn])
                    else:
                        pm_take()
                    w, n = (WP, D) if kind == "proj" else (WG, E)
                    for t in range(2):
                        for blk in range(DB):
                            last = nc.tensor.matmul(bank_of(step)[:, t * n:(t + 1) * n], ts_of(step)[:, t, blk, :], w[:, blk, :],
                                                    start=(blk == 0), stop=(blk == DB - 1))
                    last.then_inc(pm_full, 1)
                elif kind == "rank":
                    t0, t1, before = routed(*step[1:])
                    bank_, n = bank_of(step), (t1 - t0) * E
                    pe.wait_ge(sel_ready, before + 1)
                    if step in tail:
                        use[0] += 1
                    else:
                        pm_take()
                    nc.tensor.matmul(bank_[:, 0:n], CB[:, C_UP:C_UP + P],
                                     AB[:, t0:t1, :].rearrange("p t e -> p (t e)"),
                                     start=True, stop=False, skip_group_check=True)
                    nc.tensor.matmul(bank_[:, 0:n], CB[:, C_ONE:C_ONE + P],
                                     AC[:, t0:t1, :].rearrange("p t e -> p (t e)"),
                                     start=False, stop=False, skip_group_check=True)
                    nc.tensor.matmul(bank_[:, n:n + E], CB[:, C_ONE:C_ONE + P], AC[:, t1, :],
                                     start=False, stop=True, skip_group_check=True).then_inc(pm_full, 1)

            def turn_x(j, r):
                pe.wait_ge(xi_in[r % 4], 4 * (j - r % 4) + 16)
                xi = XI[:, r % 4, 0:D].bitcast(F16)
                for blk in range(2 * DB):
                    last = nc.tensor.transpose(PXT[:, 0:D].bitcast(F16)[:, blk * P:(blk + 1) * P],
                                               xi[:, blk * P:(blk + 1) * P], IDH[:, :])
                last.then_inc(f_xt, 1)

            def expert(j):
                return pe.value_load(TX[0:1, 1, bass.ds(j, 1)], min_val=0, max_val=E - 1)

            def products(bank_, turned, blocks, w, e, n, done):
                pairs = [(blk, s, t) for blk in range(blocks) for s, t in ((0, 0), (0, 1), (1, 0))]
                for i, (blk, s, t) in enumerate(pairs):
                    last = nc.tensor.matmul(bank_[:, 0:n], turned[:, s, blk, :],
                                            WF[w][:, bass.ds(e * (2 * CHUNK) + t * CHUNK + blk * n, n)],
                                            start=(i == 0), stop=(i == len(pairs) - 1))
                last.then_inc(done, 1)

            def hidden(w, bank_, e, r, done):
                products(bank_, XT[:, r % 2], DB, w, e, FI, done)

            def turn_h(j, r):
                pe.wait_ge(f_low, j + 1)
                for s in range(2):
                    for blk in range(FB):
                        at = (s * FB + blk) * P
                        last = nc.tensor.transpose(PHT[r % 2][:, :].bitcast(F16)[:, at:at + P],
                                                   HH[:, r % 2, s, blk * P:(blk + 1) * P], IDH[:, :])
                last.then_inc(f_ht, 1)

            def outputs(j, r, e):
                pe.wait_ge(f_hts, j + 1)
                pe.wait_ge(f_yo, j)
                products(PYO, HT[:, r % 2], FB, 2, e, D, f_y)

            pe.wait_ge(pm_free, use[0])
            pe.wait_ge(cb_ready, 2)
            pe.wait_ge(table_ready, 1)
            pe.wait_ge(sent, 16 * NT * TOPK)
            keep_warm(8)
            turn_x(0, 0)
            pe.wait_ge(f_xts, 1)
            turn_x(1, 1)
            pe.wait_ge(w_low, NCHUNKS)
            e0 = expert(0)
            hidden(0, P1[0], e0, 0, f_h1)
            hidden(1, P2[0], e0, 0, f_h2)

            def steady(j, r, turn=True):
                e_next = expert(j + 1)
                pe.wait_ge(f_xts, j + 2)
                hidden(0, P1[(r + 1) % 2], e_next, r + 1, f_h1)
                turn_h(j, r)
                if turn:
                    turn_x(j + 2, r + 2)
                hidden(1, P2[(r + 1) % 2], e_next, r + 1, f_h2)
                outputs(j, r, expert(j))

            n = (NTILES - 3 - 4) // 8
            for j in (0, 1, 2, 3):
                steady(j, j)
            with pe.Fori(0, n) as i:
                for r in range(8):
                    steady(8 * i + 4 + r, r)
            for j in range(8 * n + 4, NTILES - 1):
                steady(j, j % 4, turn=j + 2 < NTILES)
            j = NTILES - 1
            turn_h(j, j)
            outputs(j, j, expert(j))


_OUT = (B, T, D)


def kernel(**inputs):
    import concourse.bacc as _bacc
    from concourse.bass_utils import run_bass_kernel_spmd as _run

    a = {k: np.asarray(v) for k, v in inputs.items()}

    def rows(w, blocks):
        w = np.swapaxes(w, -1, -2)
        w = w.reshape(*w.shape[:-2], blocks, P, w.shape[-1])
        return np.ascontiguousarray(np.moveaxis(w, -2, 0))

    cst, pad = constants()
    arrays = {
        "x": np.ascontiguousarray(a["x"].reshape(NTOK, D)),
        "ctx_in": np.ascontiguousarray(a["ctx_1024"].reshape(NTOK, D)),
        "ctx_t": np.ascontiguousarray(a["ctx_1024"].reshape(NTOK, H // DB, DB, HD).transpose(3, 1, 2, 0).reshape(
            P, DB, NTOK)),
        "g_xattn": np.ascontiguousarray(a["g_xattn"]),
        "g_ffn": np.ascontiguousarray(a["g_ffn"]),
        "wp": rows(a["L0_xattn_W_proj"], DB),
        "bp": np.ascontiguousarray(a["L0_xattn_b_proj"]),
        "wg": rows(a["L0_ffn_Wg"], DB),
        "w1": rows(a["L0_ffn_W1"], DB),
        "w2": rows(a["L0_ffn_W2"], DB),
        "w3": rows(a["L0_ffn_W3"], FB),
        "cst": cst,
        "pad": pad,
        "ones": np.full((3, B // 2 * H * T // 2), 0x3F803F80, np.int32),
    }
    nc = _bacc.Bacc("TRN2", target_bir_lowering=False, num_devices=1)
    args = {k: nc.dram_tensor(k, v.shape, mybir.dt.from_np(v.dtype), kind="ExternalInput").ap()
            for k, v in arrays.items()}
    out = nc.dram_tensor("out", (NTOK, D), F32, kind="ExternalOutput").ap()
    xs = nc.dram_tensor("xs", (E * REGION + SPARE * P, ROW), F32, kind="Internal").ap()
    yt = nc.dram_tensor("yt", (SLOTS + (E + SPARE) * P, D), F32, kind="Internal").ap()
    build(nc, out=out, xs=xs, yt=yt, **args)
    r = _run(nc, [arrays], core_ids=[0])
    return r.results[0]["out"].reshape(_OUT)
```
